# Optimizing a Trainium2 kernel written in Bass

```python
import numpy as np
import jax
import jax.numpy as jnp

def _softmax(x, axis=-1):
    return jax.nn.softmax(x, axis=axis)

def _gelu(x):
    return jax.nn.gelu(x, approximate=True)

def _silu(x):
    return jax.nn.silu(x)

def _sigmoid(x):
    return jax.nn.sigmoid(x)

def _layernorm(x, axis=-1, eps=1e-05):
    m = jnp.mean(x, axis=axis, keepdims=True)
    v = jnp.var(x, axis=axis, keepdims=True)
    return (x - m) / jnp.sqrt(v + eps)

def _scatter_add(tgt, idx, src, axis=0):
    return tgt.at[idx].add(src)

def _segment_sum(src, seg, n):
    return jax.ops.segment_sum(src, seg, n)
kernel_name = 'mk_flamingo_gated_d2_seqx_r8_8bfa4c'

def setup_inputs(seed: int=0):
    np.random.seed(seed)
    _w = jnp.asarray

    def _rec_inputs():
        import jax
        import jax.numpy as jnp
        _rk = jax.random.key(seed)
        x = -7.109e-05 + 0.9999 * jax.random.normal(jax.random.fold_in(_rk, 1), (4, 256, 256), jnp.float32)
        _lenS = 256 - jax.random.randint(jax.random.fold_in(_rk, 7), (4,), 0, max(1, 256 // 4) + 1, jnp.int32)
        _lenS2 = 256 - jax.random.randint(jax.random.fold_in(_rk, 8), (4,), 0, max(1, 256 // 4) + 1, jnp.int32)
        _ctx_512P = jax.random.normal(jax.random.fold_in(_rk, 11), (4, 16, 64), jnp.float32)
        _ctx_512c = jax.random.dirichlet(jax.random.fold_in(_rk, 511), 0.3 * jnp.ones((16,), jnp.float32), (4, 256))
        _ctx_512t = jnp.einsum('bsk,bkd->bsd', _ctx_512c, _ctx_512P)
        _ctx_512t = _ctx_512t * jax.lax.rsqrt(jnp.mean(jnp.square(_ctx_512t)) + 1e-12) * 0.953939
        ctx_512 = 2.81802e-05 + 1.00001 * (_ctx_512t + 0.3 * jax.random.normal(jax.random.fold_in(_rk, 611), (4, 256, 64), jnp.float32))
        _g = jax.random.normal(jax.random.fold_in(_rk, 9001), (2, 2), jnp.float32)
        _g = jnp.sign(_g) * jnp.maximum(jnp.abs(_g), 1.0) + (_g == 0) * 1.0
        g_xattn = _g[0]
        g_ffn = _g[1]
        return (x, ctx_512, g_xattn, g_ffn)
    x, ctx_512, g_xattn, g_ffn = _rec_inputs()

    def _L0_xattn_setup():
        import jax, jax.numpy as jnp
        import numpy as np
        EPS = 1e-06
        IMAGE_DIMS = 256
        key = jax.random.key(seed)
        k1, k2, k3 = jax.random.split(key, 3)
        B, I, J, D = (16, 256, 256, 64)
        p = jax.random.normal(k1, (B, I, J), dtype=jnp.float32)
        k_v = jax.random.normal(k2, (B, J, D), dtype=jnp.float32)
        W_k = jax.random.normal(k3, (D, D), dtype=jnp.float32) * (1.0 / np.sqrt(D))
        b_k = jnp.zeros((D,), dtype=jnp.float32)
        ln_gamma = jnp.ones((J,), dtype=jnp.float32)
        ln_beta = jnp.zeros((J,), dtype=jnp.float32)
        return {'p': p, 'k_v': k_v, 'W_k': W_k, 'b_k': b_k, 'ln_gamma': ln_gamma, 'ln_beta': ln_beta}
    _L0_xattn_all = _L0_xattn_setup()
    _L0_xattn_in = {k: v for k, v in _L0_xattn_all.items() if k in ('W_k', 'b_k', 'ln_gamma', 'ln_beta')}
    del _L0_xattn_all

    def _L0_ffn_setup():
        import jax, jax.numpy as jnp
        import numpy as np
        D_MODEL = 256
        HIDDEN = 4 * D_MODEL
        B, S = (2, 512)

        def bit_linear(x, w, b):
            gamma_x = jnp.clip(jnp.max(jnp.abs(x), axis=-1, keepdims=True), 1e-05, None)
            scale_x = 127.0 / gamma_x
            x_dq = jnp.clip(jnp.round(x * scale_x), -128.0, 127.0) / scale_x
            x_ste = x + jax.lax.stop_gradient(x_dq - x)
            gamma_w = jnp.clip(jnp.mean(jnp.abs(w)), 1e-05, None)
            w_dq = jnp.clip(jnp.round(w / gamma_w), -1.0, 1.0) * gamma_w
            w_ste = w + jax.lax.stop_gradient(w_dq - w)
            return jnp.einsum('bsd,hd->bsh', x_ste, w_ste) + b
        key = jax.random.key(seed)
        ks = jax.random.split(key, 7)
        std = 0.02
        return {'x': jax.random.normal(ks[0], (B, S, D_MODEL), dtype=jnp.float32), 'gate_w': jax.random.normal(ks[1], (HIDDEN, D_MODEL), dtype=jnp.float32) * std, 'gate_b': jnp.zeros((HIDDEN,), dtype=jnp.float32), 'val_w': jax.random.normal(ks[2], (HIDDEN, D_MODEL), dtype=jnp.float32) * std, 'val_b': jnp.zeros((HIDDEN,), dtype=jnp.float32), 'out_w': jax.random.normal(ks[3], (D_MODEL, HIDDEN), dtype=jnp.float32) * std, 'out_b': jnp.zeros((D_MODEL,), dtype=jnp.float32)}
    _L0_ffn_all = _L0_ffn_setup()
    _L0_ffn_in = {k: v for k, v in _L0_ffn_all.items() if k in ('gate_w', 'gate_b', 'val_w', 'val_b', 'out_w', 'out_b')}
    del _L0_ffn_all

    def _L1_xattn_setup():
        import jax, jax.numpy as jnp
        import numpy as np
        B, S, L = (2, 128, 128)
        DIM_Q, H, K, D_C, D_CQ, R = (256, 16, 128, 64, 192, 64)

        def _rope_tables(length, dim):
            inv = 1.0 / 10000.0 ** (jnp.arange(0, dim, 2, dtype=jnp.float32) / dim)
            f = jnp.arange(length, dtype=jnp.float32)[:, None] * inv[None, :]
            sin = jnp.repeat(jnp.sin(f), 2, axis=-1)
            cos = jnp.repeat(jnp.cos(f), 2, axis=-1)
            return (sin, cos)

        def _rotate_half(x):
            half = x.shape[-1] // 2
            return jnp.concatenate([-x[..., half:], x[..., :half]], axis=-1)

        def _apply_rope(x, sin, cos):
            return x * cos + _rotate_half(x) * sin
        key = jax.random.key(seed)
        ks = jax.random.split(key, 8)
        return {'hidden_q': jax.random.normal(ks[0], (B, S, DIM_Q), jnp.float32), 'kv_c': jax.random.normal(ks[1], (B, L, D_C), jnp.float32), 'Wq': jax.random.normal(ks[2], (H * K, DIM_Q), jnp.float32) / np.sqrt(DIM_Q).astype(np.float32), 'w_kc_q': jax.random.normal(ks[3], (H, K, D_CQ), jnp.float32) / np.sqrt(K).astype(np.float32), 'w_kc_kv': jax.random.normal(ks[4], (H, K, D_C), jnp.float32) / np.sqrt(K).astype(np.float32), 'W_qr': jax.random.normal(ks[5], (H, D_CQ, R), jnp.float32) / np.float32(np.sqrt(D_CQ) * np.sqrt(R)), 'W_kr': jax.random.normal(ks[6], (H, D_C, R), jnp.float32) / np.sqrt(D_C).astype(np.float32), 'Wo': jax.random.normal(ks[7], (DIM_Q, H * K), jnp.float32) / np.sqrt(H * K).astype(np.float32)}
    _L1_xattn_all = _L1_xattn_setup()
    _L1_xattn_in = {k: v for k, v in _L1_xattn_all.items() if k in ('Wq', 'w_kc_q', 'w_kc_kv', 'W_qr', 'W_kr', 'Wo')}
    del _L1_xattn_all

    def _L1_ffn_setup():
        import math
        import jax, jax.numpy as jnp
        import numpy as np
        NUM_EXPERTS = 8
        TOP_K = 2
        CAP_FACTOR = 1.25
        D_MODEL = 256
        D_HIDDEN = 1024
        B, S = (4, 256)
        key = jax.random.key(seed)
        ks = jax.random.split(key, 6)
        x = jax.random.normal(ks[0], (B, S, D_MODEL), dtype=jnp.float32)
        gating_w = jax.random.normal(ks[1], (D_MODEL, NUM_EXPERTS), dtype=jnp.float32) * (1.0 / math.sqrt(D_MODEL))
        w1 = jax.random.normal(ks[2], (NUM_EXPERTS, D_MODEL, D_HIDDEN), dtype=jnp.float32) * (1.0 / math.sqrt(D_MODEL))
        b1 = jnp.zeros((NUM_EXPERTS, D_HIDDEN), dtype=jnp.float32)
        w2 = jax.random.normal(ks[3], (NUM_EXPERTS, D_HIDDEN, D_MODEL), dtype=jnp.float32) * (1.0 / math.sqrt(D_HIDDEN))
        b2 = jnp.zeros((NUM_EXPERTS, D_MODEL), dtype=jnp.float32)
        return {'x': x, 'gating_w': gating_w, 'w1': w1, 'b1': b1, 'w2': w2, 'b2': b2}
    _L1_ffn_all = _L1_ffn_setup()
    _L1_ffn_in = {k: v for k, v in _L1_ffn_all.items() if k in ('gating_w', 'w1', 'b1', 'w2', 'b2')}
    del _L1_ffn_all
    return {'x': x, 'ctx_512': ctx_512, 'g_xattn': g_xattn, 'g_ffn': g_ffn, 'L0_xattn_W_k': _L0_xattn_in['W_k'], 'L0_xattn_b_k': _L0_xattn_in['b_k'], 'L0_xattn_ln_gamma': _L0_xattn_in['ln_gamma'], 'L0_xattn_ln_beta': _L0_xattn_in['ln_beta'], 'L0_ffn_gate_w': _L0_ffn_in['gate_w'], 'L0_ffn_gate_b': _L0_ffn_in['gate_b'], 'L0_ffn_val_w': _L0_ffn_in['val_w'], 'L0_ffn_val_b': _L0_ffn_in['val_b'], 'L0_ffn_out_w': _L0_ffn_in['out_w'], 'L0_ffn_out_b': _L0_ffn_in['out_b'], 'L1_xattn_Wq': _L1_xattn_in['Wq'], 'L1_xattn_w_kc_q': _L1_xattn_in['w_kc_q'], 'L1_xattn_w_kc_kv': _L1_xattn_in['w_kc_kv'], 'L1_xattn_W_qr': _L1_xattn_in['W_qr'], 'L1_xattn_W_kr': _L1_xattn_in['W_kr'], 'L1_xattn_Wo': _L1_xattn_in['Wo'], 'L1_ffn_gating_w': _L1_ffn_in['gating_w'], 'L1_ffn_w1': _L1_ffn_in['w1'], 'L1_ffn_b1': _L1_ffn_in['b1'], 'L1_ffn_w2': _L1_ffn_in['w2'], 'L1_ffn_b2': _L1_ffn_in['b2']}

def reference(x, ctx_512, g_xattn, g_ffn, L0_xattn_W_k, L0_xattn_b_k, L0_xattn_ln_gamma, L0_xattn_ln_beta, L0_ffn_gate_w, L0_ffn_gate_b, L0_ffn_val_w, L0_ffn_val_b, L0_ffn_out_w, L0_ffn_out_b, L1_xattn_Wq, L1_xattn_w_kc_q, L1_xattn_w_kc_kv, L1_xattn_W_qr, L1_xattn_W_kr, L1_xattn_Wo, L1_ffn_gating_w, L1_ffn_w1, L1_ffn_b1, L1_ffn_w2, L1_ffn_b2):
    import jax
    import jax.numpy as jnp

    def _L0_xattn_ref(p, k_v, W_k, b_k, ln_gamma, ln_beta):
        import jax, jax.numpy as jnp
        import numpy as np
        EPS = 1e-06
        IMAGE_DIMS = 256
        kv = k_v @ W_k.T + b_k
        out = jnp.einsum('bij,bjd->bid', p, kv)
        scale = IMAGE_DIMS ** (-0.5)
        sim = jnp.einsum('bid,bjd->bij', out, kv) * scale
        mu = jnp.mean(sim, axis=-1, keepdims=True)
        var = jnp.var(sim, axis=-1, keepdims=True)
        sim = (sim - mu) * jax.lax.rsqrt(var + EPS) * ln_gamma + ln_beta
        attn = jax.nn.softmax(sim, axis=-1)
        return attn

    def _L0_ffn_ref(x, gate_w, gate_b, val_w, val_b, out_w, out_b):
        import jax, jax.numpy as jnp
        import numpy as np
        D_MODEL = 256
        HIDDEN = 4 * D_MODEL
        B, S = (2, 512)

        def bit_linear(x, w, b):
            gamma_x = jnp.clip(jnp.max(jnp.abs(x), axis=-1, keepdims=True), 1e-05, None)
            scale_x = 127.0 / gamma_x
            x_dq = jnp.clip(jnp.round(x * scale_x), -128.0, 127.0) / scale_x
            x_ste = x + jax.lax.stop_gradient(x_dq - x)
            gamma_w = jnp.clip(jnp.mean(jnp.abs(w)), 1e-05, None)
            w_dq = jnp.clip(jnp.round(w / gamma_w), -1.0, 1.0) * gamma_w
            w_ste = w + jax.lax.stop_gradient(w_dq - w)
            return jnp.einsum('bsd,hd->bsh', x_ste, w_ste) + b
        gate = jax.nn.silu(bit_linear(x, gate_w, gate_b))
        val = bit_linear(x, val_w, val_b)
        return bit_linear(gate * val, out_w, out_b)

    def _L1_xattn_ref(hidden_q, kv_c, Wq, w_kc_q, w_kc_kv, W_qr, W_kr, Wo):
        import jax, jax.numpy as jnp
        import numpy as np
        B, S, L = (2, 128, 128)
        DIM_Q, H, K, D_C, D_CQ, R = (256, 16, 128, 64, 192, 64)

        def _rope_tables(length, dim):
            inv = 1.0 / 10000.0 ** (jnp.arange(0, dim, 2, dtype=jnp.float32) / dim)
            f = jnp.arange(length, dtype=jnp.float32)[:, None] * inv[None, :]
            sin = jnp.repeat(jnp.sin(f), 2, axis=-1)
            cos = jnp.repeat(jnp.cos(f), 2, axis=-1)
            return (sin, cos)

        def _rotate_half(x):
            half = x.shape[-1] // 2
            return jnp.concatenate([-x[..., half:], x[..., :half]], axis=-1)

        def _apply_rope(x, sin, cos):
            return x * cos + _rotate_half(x) * sin
        Bv, Sv, _ = hidden_q.shape
        _, Lv, _ = kv_c.shape
        q_hk = (hidden_q @ Wq.T).reshape(Bv, Sv, H, K)
        q_big = jnp.einsum('bshk,hkq->bshq', q_hk, w_kc_q)
        sin_q, cos_q = _rope_tables(Sv, D_CQ)
        q_big = _apply_rope(q_big, sin_q[None, :, None, :], cos_q[None, :, None, :])
        sin_k, cos_k = _rope_tables(Lv, D_C)
        kv_r = _apply_rope(kv_c, sin_k[None], cos_k[None])
        q_r = jnp.einsum('bshq,hqr->bhsr', q_big, W_qr)
        k_r = jnp.einsum('bld,hdr->bhlr', kv_r, W_kr)
        scores = jnp.einsum('bhsr,bhlr->bhsl', q_r, k_r)
        attn = jax.nn.softmax(scores, axis=-1)
        ctx_c = jnp.einsum('bhsl,bld->bhsd', attn, kv_r)
        ctx_lat = jnp.einsum('bhsd,hkd->bhsk', ctx_c, w_kc_kv)
        ctx = ctx_lat.transpose(0, 2, 1, 3).reshape(Bv, Sv, H * K)
        return ctx @ Wo.T

    def _L1_ffn_ref(x, gating_w, w1, b1, w2, b2):
        import math
        import jax, jax.numpy as jnp
        import numpy as np
        NUM_EXPERTS = 8
        TOP_K = 2
        CAP_FACTOR = 1.25
        D_MODEL = 256
        D_HIDDEN = 1024
        B, S = (4, 256)
        b, s, d = x.shape
        x_flat = x.reshape(-1, d)
        T = x_flat.shape[0]
        num_items = T * TOP_K
        capacity = int(math.ceil(num_items / NUM_EXPERTS * CAP_FACTOR))
        gates = jax.nn.softmax(x_flat @ gating_w, axis=-1)
        topk_w, topk_idx = jax.lax.top_k(gates, TOP_K)
        norm_w = topk_w / (jnp.sum(topk_w, axis=-1, keepdims=True) + 1e-08)
        flat_e = topk_idx.reshape(-1)
        flat_t = jnp.repeat(jnp.arange(T, dtype=jnp.int32), TOP_K)
        flat_w = norm_w.reshape(-1)
        onehot = (flat_e[:, None] == jnp.arange(NUM_EXPERTS)[None, :]).astype(jnp.int32)
        pos_all = jnp.cumsum(onehot, axis=0) - 1
        position = jnp.take_along_axis(pos_all, flat_e[:, None].astype(jnp.int32), axis=1)[:, 0]
        valid = position < capacity
        pos_scatter = jnp.where(valid, position, capacity)
        buf = jnp.zeros((NUM_EXPERTS, capacity, d), dtype=x.dtype)
        buf = buf.at[flat_e, pos_scatter].set(x_flat[flat_t], mode='drop')
        h = jnp.maximum(jnp.einsum('ecd,edh->ech', buf, w1) + b1[:, None, :], 0.0)
        out_e = jnp.einsum('ech,ehd->ecd', h, w2) + b2[:, None, :]
        pos_gather = jnp.minimum(position, capacity - 1)
        gathered = out_e[flat_e, pos_gather]
        w_eff = jnp.where(valid, flat_w, 0.0)
        out_flat = jnp.zeros_like(x_flat).at[flat_t].add(gathered * w_eff[:, None])
        return out_flat.reshape(b, s, d)
    x = x + jnp.tanh(g_xattn[0]) * _L0_xattn_ref(_layernorm(x, axis=-1), ctx_512, L0_xattn_W_k, L0_xattn_b_k, L0_xattn_ln_gamma, L0_xattn_ln_beta)
    x = x + jnp.tanh(g_ffn[0]) * _L0_ffn_ref(_layernorm(x, axis=-1), L0_ffn_gate_w, L0_ffn_gate_b, L0_ffn_val_w, L0_ffn_val_b, L0_ffn_out_w, L0_ffn_out_b)
    x = x + jnp.tanh(g_xattn[1]) * _L1_xattn_ref(_layernorm(x, axis=-1), ctx_512, L1_xattn_Wq, L1_xattn_w_kc_q, L1_xattn_w_kc_kv, L1_xattn_W_qr, L1_xattn_W_kr, L1_xattn_Wo)
    x = x + jnp.tanh(g_ffn[1]) * _L1_ffn_ref(_layernorm(x, axis=-1), L1_ffn_gating_w, L1_ffn_w1, L1_ffn_b1, L1_ffn_w2, L1_ffn_b2)
    return x

_drawn_inputs = setup_inputs


def setup_inputs(seed=0):
    import zlib

    import numpy as np

    out = dict(_drawn_inputs(seed))
    spreads = {'g_ffn': (-1.0, 0.537),
     'L0_xattn_b_k': (0.0, 0.8),
     'L0_xattn_ln_gamma': (1.0, 0.6),
     'L0_xattn_ln_beta': (0.0, 0.8),
     'L0_ffn_gate_b': (0.0, 0.526),
     'L0_ffn_val_b': (0.0, 0.342),
     'L0_ffn_out_b': (0.0, 0.1),
     'L1_ffn_b1': (0.0, 0.1),
     'L1_ffn_b2': (0.0, 0.1)}
    factors = {'L0_xattn_W_k': 8.0}
    for name, (base, spread) in spreads.items():
        noise = np.random.default_rng([zlib.crc32(name.encode()), seed]).standard_normal(out[name].shape)
        drawn = base * np.exp(spread * noise) if base else spread * noise
        out[name] = jnp.asarray(drawn.astype(out[name].dtype))
    for name, factor in factors.items():
        out[name] = (out[name] * factor).astype(out[name].dtype)
    return out
```

```python
from contextlib import ExitStack

import numpy as np
import concourse.bass as bass
from concourse import mybir

ALU = mybir.AluOpType
ACT = mybir.ActivationFunctionType
AX = mybir.AxisListType
F32 = mybir.dt.float32
F16 = mybir.dt.float16
BF16 = mybir.dt.bfloat16
U32 = mybir.dt.uint32

P = 128
B, S, D = 4, 256, 256
T = B * S
NT = T // P
TPB = S // P
KC = D // P
DC = 64
FH = 4 * D
NH, HK, DCQ = 16, 128, 192
HALF = DCQ // 2
G = 4
NG = NH // G
QT = G * HALF // P
NGB = B * NG
NHB = B * NH
NE, TOPK, EH = 8, 2, 1024
MH = EH // P
CAP = -(-T * TOPK * 5 // (NE * 4))
SLOTS = NE * CAP
WS = 64.0
MAGIC = 12582912.0
PASSES = ((0, 0), (0, 1), (1, 0))
STAGE = 9


def program(nc, A, out):
    ctx = ExitStack()
    with ctx:
        def sb(name, shape, dt=F32):
            return ctx.enter_context(nc.sbuf_tensor(name, shape, dt))

        def sem(name):
            return ctx.enter_context(nc.semaphore(name))

        def carve(arena, kb):
            at = [0]

            def take(shape, dt=F32):
                n = int(np.prod(shape)) * (4 if dt in (F32, U32) else 2) // 4
                a = arena[:, at[0]:at[0] + n]
                at[0] += n
                assert at[0] <= kb * 256, (at[0], kb)
                if dt != F32:
                    a = a.bitcast(dt)
                if len(shape) == 2:
                    a = a.rearrange("p (a b) -> p a b", a=shape[0])
                if len(shape) == 3:
                    a = a.rearrange("p (a b c) -> p a b c", a=shape[0], b=shape[1])
                return a
            return take

        bank = [ctx.enter_context(nc.psum_tensor(f"bank{i}", [P, 512], F32)) for i in range(8)]

        x_sb = sb("x_sb", [P, NT, D])
        y_sb = sb("y_sb", [P, NT, D])
        identf = sb("identf", [P, P])
        ident16 = sb("ident16", [P, P], F16)
        identb = sb("identb", [P, P], BF16)
        onesf = sb("onesf", [P, P])
        ctx_n = sb("ctx_n", [P, NT, DC])
        gx = sb("gx", [P, 2])
        gf = sb("gf", [P, 2])
        tgx = sb("tgx", [P, 2])
        tgf = sb("tgf", [P, 2])
        tgx1 = sb("tgx1", [P, 1])
        stats = sb("stats", [P, NT, 6])
        mv = sb("mv", [P, NT, 2])
        vareps = sb("vareps", [P, NT])
        mhalf = sb("mhalf", [P, NT])
        magic = sb("magic", [P, 1])
        rstd = sb("rstd", [P, NT])

        lp = carve(sb("lp", [P, 74 * 256]), 74)
        yt_f = lp([KC, T])
        yth = yt_f[:, 0, :].bitcast(F16).rearrange("p (a b) -> p a b", a=KC)
        ytl = yt_f[:, 1, :].bitcast(F16).rearrange("p (a b) -> p a b", a=KC)
        m1 = [lp([KC, 2, NH * HALF], F16) for _ in range(2)]
        zp = lp([NG * 2 * 4, P])
        nn = [lp([NH // 2, D], F16) for _ in range(2)]
        tabs = lp([2 * QT * 2 * S])
        cosq, sinq = [tabs[:, i * 2 * QT * S:(i + 1) * 2 * QT * S].rearrange("p (a b) -> p a b", a=QT) for i in range(2)]
        kvt = [lp([T], F16) for _ in range(2)]
        kvr = [lp([NT, DC], F16) for _ in range(2)]

        lw = sb("lw", [P, 34 * 256])
        se = sb("se", [P, 69 * 256])
        w0 = carve(lw, 34)
        outT = w0([T])
        kv0 = w0([NT, DC])
        kvT0 = w0([T])
        ctxT = w0([T])
        wkT = w0([DC])
        bkc = w0([1])
        bkb = w0([DC])
        gab = w0([D])
        beb = w0([D])
        z_sb = w0([NT, D])
        w0([30 * 256 - (2 * T + T + 512 + 64 + 1 + 64 + 2 * D + NT * D)])
        st_sb = w0([2, 512])
        stats2 = sb("stats2", [P, NT, 6])
        mv2 = sb("mv2", [P, NT, 2])
        ve2 = sb("ve2", [P, NT])
        rstd2 = sb("rstd2", [P, NT])
        nm0 = sb("nm0", [P, NT])
        sum0 = sb("sum0", [P, NT])
        r0 = sb("r0", [P, NT])
        w1 = carve(lw, 34)
        g_sb = w1([2, FH])
        v_sb = w1([2, FH])
        hq = w1([2, FH], BF16)
        hqT = w1([2, FH], BF16)
        q_sb = w1([NT, D], BF16)
        qT = w1([2, D], BF16)
        fo = w1([D])
        w2 = carve(lw, 34)
        raw = w2([2, 512])
        t1 = w2([2, 512])
        t2 = w2([2, 512])
        rope = w2([QT, 512])
        qz = [w2([2, 512], F16) for _ in range(2)]
        e_sb = w2([2, 512])
        at = [w2([2, 512], F16) for _ in range(2)]
        cxn = w2([512])
        ct = [w2([512], F16) for _ in range(2)]
        kvdup = raw.rearrange("p a b -> p (a b)").rearrange("p (t j d) -> p t j d", t=NT, j=2)
        nmax = sb("nmax", [P, 2, TPB])
        esum = sb("esum", [P, 2, TPB, G])
        rsum = sb("rsum", [P, 2, TPB, G])
        kcos = sb("kcos", [P, TPB, DC])
        ksin = sb("ksin", [P, TPB, DC])
        s1 = carve(se, 69)
        r1 = s1([28 * 256])
        r2 = s1([20 * 256])
        gb_b = s1([FH])
        vb_b = s1([FH])
        ob_b = s1([D])
        gtern = s1([KC, FH], BF16)
        vtern = s1([KC, FH], BF16)
        otern = s1([FH // P, D], BF16)
        wraw = [r1[:, 2048 * i:2048 * (i + 1)] for i in range(3)]
        wq = zp.rearrange("p a b -> p (a b)").rearrange("p (a b) -> p a b", a=NH)
        kcq = tabs.rearrange("p (a b) -> p a b", a=NH)
        zl = r1[:, 0:4096].rearrange("p (a b) -> p a b", a=NG * 2 * 4)
        zr = r1[:, 4096:5120].rearrange("p (a b) -> p a b", a=NH // 2)
        woT = r2[:, 0:4096].rearrange("p (a b) -> p a b", a=NH)
        kckv = r2[:, 4096:5120].rearrange("p (a b) -> p a b", a=NH)
        wabs = sb("wabs", [P, 3])
        gw = sb("gw", [P, 3])
        thr = sb("thr", [P, 3])
        nthr = sb("nthr", [P, 3])
        am = sb("am", [P, NT])
        qs = sb("qs", [P, NT])
        sgs = sb("sgs", [P, NT])
        svs = sb("svs", [P, NT])
        am2 = sb("am2", [P, NT])
        qs2 = sb("qs2", [P, NT])
        sos = sb("sos", [P, NT])
        s3 = carve(se, 69)
        eraw = s3([2, KC * EH])
        we = [[s3([2, KC * EH], F16) for _ in range(2)] for _ in range(2)]
        b2b = s3([NE, D])
        got = eraw.rearrange("p a b -> p (a b)").rearrange("p (t k) -> p t k", t=NT)
        w3 = carve(lw, 34)
        rows = w3([NT, 2 * D], F16)
        slots = w3([3, 2 * D], F16)
        bufT = w3([2, KC * CAP], F16)
        hs = [w3([MH, CAP], F16) for _ in range(2)]
        hr = w3([2, CAP])
        oe = w3([6, D])
        b1s = sb("b1s", [P, NE * MH])
        b1w = sb("b1w", [P, NE * MH])
        gwt = sb("gwt", [P, KC, NE])
        trib = sb("trib", [P, P], BF16)
        onesb = sb("onesb", [P, P], BF16)
        iota8 = sb("iota8", [P, NE])
        spare = sb("spare", [P, 1])
        mx = sb("mx", [P, NT])
        el = sb("el", [P, NT, NE])
        es = sb("es", [P, NT])
        gates = sb("gates", [P, NT, NE])
        v8 = sb("v8", [P, NT, 8])
        i8 = sb("i8", [P, NT, 8], U32)
        idf = sb("idf", [P, NT, TOPK])
        oh = sb("oh", [P, NT, TOPK, NE])
        ohs = sb("ohs", [P, NT, NE], BF16)
        pr = sb("pr", [P, NT, TOPK, NE])
        pos = sb("pos", [P, NT, TOPK])
        val = sb("val", [P, NT, TOPK])
        base = sb("base", [P, NT, TOPK])
        sl = sb("sl", [P, NT, TOPK])
        sl2 = sb("sl2", [P, NT, TOPK])
        scat = sb("scat", [P, NT * TOPK], U32)
        gi = sb("gi", [P, NT, TOPK])
        gidx = sb("gidx", [P, NT * TOPK], U32)
        ws = sb("ws", [P, NT])
        wn = sb("wn", [P, NT, TOPK])
        zero = kvt[0][:, 0:2 * D]
        buf_d = nc.dram_tensor("dispatch", (SLOTS + P, 2 * D), F16).ap()
        oe_d = nc.dram_tensor("expert_rows", (SLOTS, D), F32).ap()

        x_v = A["x"].rearrange("b (h p) d -> p (b h) d", p=P)
        out_v = out.rearrange("b (h p) d -> p (b h) d", p=P)

        d_x, d_c, d_k, d_w, d_gb = sem("d_x"), sem("d_c"), sem("d_k"), sem("d_w"), sem("d_gb")
        d_n, d_m, d_z, d_t = sem("d_n"), sem("d_m"), sem("d_z"), sem("d_t")
        d_e, d_b, d_zero, d_scat, d_slot = sem("d_e"), sem("d_b"), sem("d_zero"), sem("d_scat"), sem("d_slot")
        d_oe, d_got, d_out = [sem(f"d_oe{i}") for i in range(6)], [sem(f"d_got{t}") for t in range(NT)], sem("d_out")
        c_dve, c_pool, c_act = sem("c_dve"), sem("c_pool"), sem("c_act")
        s_init = sem("s_init")
        s_stat, s_rstd, s_upd = sem("s_stat"), sem("s_rstd"), sem("s_upd")
        s_tanh = sem("s_tanh")
        p_kvT, a_kvT, p_kv, v_kv = sem("p_kvT"), sem("a_kvT"), sem("p_kv"), sem("v_kv")
        v_y0, p_yT0, a_yT0, p_oT, a_oT = sem("v_y0"), sem("p_yT0"), sem("a_yT0"), sem("p_oT"), sem("a_oT")
        p_sim, v_sst, g_srs, v_z, g_z, v_nm0, a_exp0 = (sem("p_sim"), sem("v_sst"), sem("g_srs"), sem("v_z"),
                                                       sem("g_z"), sem("v_nm0"), sem("a_exp0"))
        a_abs, p_abs, v_tern = sem("a_abs"), sem("p_abs"), sem("v_tern")
        v_q, p_qT, a_qT, p_gv, v_gv, a_silu = sem("v_q"), sem("p_qT"), sem("a_qT"), sem("p_gv"), sem("v_gv"), sem("a_silu")
        v_hq, p_hT, a_hT, p_fo, v_fo = sem("v_hq"), sem("p_hT"), sem("a_hT"), sem("p_fo"), sem("v_fo")
        v_qs2, a_rnd = sem("v_qs2"), sem("a_rnd")
        p_set, a_raws, a_set, g_set = sem("p_set"), sem("a_raws"), sem("a_set"), sem("g_set")
        v_y2, p_yT2, a_yT2, v_yT2 = sem("v_y2"), sem("p_yT2"), sem("a_yT2"), sem("v_yT2")
        v_kr, p_kr, a_kr, v_krl = sem("v_kr"), sem("p_kr"), sem("a_kr"), sem("v_krl")
        p_qb, a_raw, v_t1, g_t2, g_rope = sem("p_qb"), sem("a_raw"), sem("v_t1"), sem("g_t2"), sem("g_rope")
        p_qz, a_qz, v_qz = sem("p_qz"), sem("a_qz"), sem("v_qz")
        p_sc, v_max, a_exp, p_at, a_at, v_at, p_cx = (sem("p_sc"), sem("v_max"), sem("a_exp"), sem("p_at"),
                                                     sem("a_at"), sem("v_at"), sem("p_cx"))
        v_norm, p_ct, a_ct, v_ct, p_out = sem("v_norm"), sem("p_ct"), sem("a_ct"), sem("v_ct"), sem("p_out")
        v_y3, g_row, p_yT3, a_yT3, p_lg = sem("v_y3"), sem("g_row"), sem("p_yT3"), sem("a_yT3"), sem("p_lg")
        v_el, a_el, v_oh, p_pos, v_idx = sem("v_el"), sem("a_el"), sem("v_oh"), sem("p_pos"), sem("v_idx")
        a_we, v_we = sem("a_we"), sem("v_we")
        p_bT, a_bT, v_bT = sem("p_bT"), sem("a_bT"), sem("v_bT")
        p_h, a_h, v_h, g_h, p_oe, v_oe = sem("p_h"), sem("a_h"), sem("v_h"), sem("g_h"), sem("p_oe"), sem("v_oe")
        v_fin = sem("v_fin")

        NSET = NH // 2 + NH + 8
        KB = NH // 2 + NH

        def unit(u):
            w = KC * DCQ if u < NH else D
            bk, st = bank[4 + u % 4][:, 0:w], st_sb[:, u % 2, 0:w]
            if u >= NH:
                return bk, st, [n[:, u - NH, :] for n in nn]
            bk, st = [x.rearrange("p (a b c) -> p a b c", a=KC, b=2) for x in (bk, st)]
            return bk, st, [m[:, :, :, u * HALF:(u + 1) * HALF] for m in m1]

        def tiles_at(n):
            g, h = n // G, n % G
            return [c for c in {2: [QT * (g + 2)], 3: [QT * (g + 2) + 1, QT * (g + 2) + 2]}.get(h, []) if c < QT * NGB]

        block = ctx.enter_context(nc.Block())

        @block.sync
        def _(sp):
            for h in range(2):
                sp.dma_start(x_sb[:, 4 * h:4 * h + 4, :], x_v[:, 4 * h:4 * h + 4, :]).then_inc(d_x, 16)
            sp.dma_start(wraw[0].rearrange("p (a b) -> p a b", a=KC),
                         A["gate_wT"].rearrange("(a p) n -> p a n", p=P)).then_inc(d_w, 16)
            sp.wait_ge(d_w, 16)
            sp.dma_start(wraw[1].rearrange("p (a b) -> p a b", a=KC),
                         A["val_wT"].rearrange("(a p) n -> p a n", p=P)).then_inc(d_w, 16)
            sp.wait_ge(d_w, 32)
            sp.dma_start(wraw[2].rearrange("p (a b) -> p a b", a=FH // P),
                         A["out_wT"].rearrange("(a p) n -> p a n", p=P)).then_inc(d_w, 16)
            for dst, name in ((gb_b, "gate_b"), (vb_b, "val_b"), (ob_b, "out_b")):
                sp.dma_start(dst, A[name].partition_broadcast(P)).then_inc(d_gb, 16)
            if STAGE >= 3:
                sp.dma_start(wq, A["Wq"].rearrange("(h k) n -> k h n", k=P)).then_inc(d_m, 16)
                sp.dma_start(kcq, A["w_kc_q"].rearrange("h k n -> k h n")).then_inc(d_m, 16)
                sp.dma_start(woT, A["WoT"].rearrange("(h k) n -> k h n", k=P)).then_inc(d_n, 16)
                sp.dma_start(kckv, A["w_kc_kv"].rearrange("h k n -> k h n")).then_inc(d_n, 16)
                sp.wait_ge(v_tern, 3)
                sp.wait_ge(a_abs, 3)
                sp.dma_start(zl, A["ZL"].rearrange("a k n -> k a n")).then_inc(d_z, 16)
                sp.dma_start(zr, A["ZR"].rearrange("a k n -> k a n")).then_inc(d_z, 16)
                sp.wait_ge(p_set, KB)
                sp.dma_start(cosq, A["cosq"]).then_inc(d_t, 16)
                sp.dma_start(sinq, A["sinq"]).then_inc(d_t, 16)
            if STAGE >= 4:
                sp.wait_ge(p_set, NSET)
                sp.wait_ge(v_fo, NT)
                sp.dma_start(b2b, A["b2"].partition_broadcast(P)).then_inc(d_b, 16)

                def weights(e):
                    if e >= 1:
                        sp.wait_ge(v_we, 4 * e)
                    sp.dma_start(eraw[:, 0, :].rearrange("p (a b) -> p a b", a=KC),
                                 A["w1"][e].rearrange("(a p) n -> p a n", p=P)).then_inc(d_e, 16)
                    sp.dma_start(eraw[:, 1, :].rearrange("p (a b) -> p a b", a=MH),
                                 A["w2"][e].rearrange("(a p) n -> p a n", p=P)).then_inc(d_e, 16)

                def dispatched(e):
                    if e == 0:
                        sp.wait_ge(d_scat, 16 * NT * TOPK)
                    else:
                        sp.wait_ge(p_bT, 2 * e)
                    sp.dma_start(slots[:, 0:2, :], buf_d[e * CAP:e * CAP + 2 * P, :].rearrange("(a p) c -> p a c", p=P))\
                        .then_inc(d_slot, 16)
                    sp.dma_start(slots[0:CAP - 2 * P, 2, :], buf_d[e * CAP + 2 * P:(e + 1) * CAP, :]).then_inc(d_slot, 16)

                weights(0)
                weights(1)
                dispatched(0)
                for e in range(NE):
                    if e + 1 < NE:
                        dispatched(e + 1)
                    if e + 2 < NE:
                        weights(e + 2)
                    for i in range(3):
                        k = 3 * e + i
                        w = min(P, CAP - P * i)
                        sp.wait_ge(v_oe, k + 1)
                        sp.dma_start(oe_d[e * CAP + P * i:e * CAP + P * i + w, :], oe[0:w, k % 6, :])\
                            .then_inc(d_oe[k % 6], 16)
            for t in range(NT):
                sp.wait_ge(v_fin, t + 1)
                sp.dma_start(out_v[:, t, :], x_sb[:, t, :]).then_inc(d_out, 16)
            sp.wait_ge(d_out, 16 * NT)

        @block.gpsimd
        def _(pool):
            chain = [0]

            def link(ins):
                chain[0] += 1
                ins.then_inc(c_pool, 1)
                pool.wait_ge(c_pool, chain[0])

            nc.gpsimd.memset(onesf[:, :], 1.0).then_inc(s_init, 1)
            nc.gpsimd.memset(onesb[:, :], 1.0).then_inc(s_init, 1)
            nc.gpsimd.memset(zero, 0.0).then_inc(s_init, 1)
            nc.gpsimd.memset(mhalf[:, :], -0.5).then_inc(s_init, 1)
            nc.gpsimd.memset(magic[:, :], MAGIC).then_inc(s_init, 1)
            pool.wait_ge(s_init, 5)
            def inv_std(a, b, stat, src, ve, dst, eps):
                link(nc.gpsimd.tensor_scalar(ve[:, a:b], src[:, a:b, 1], eps, None, ALU.add))
                nc.gpsimd.tensor_tensor(dst[:, a:b], ve[:, a:b], mhalf[:, a:b], ALU.pow).then_inc(stat, 1)

            pool.wait_ge(s_stat, 1)
            inv_std(0, NT, s_rstd, mv, vareps, rstd, 1e-5)
            for s in range(B + 1):
                if s < B:
                    pool.wait_ge(v_sst, s + 1)
                    inv_std(TPB * s, TPB * s + TPB, g_srs, mv2, ve2, rstd2, 1e-6)
                if s >= 1:
                    b = s - 1
                    pool.wait_ge(v_z, b + 1)
                    if b == 0:
                        pool.wait_ge(d_k, 96)
                    zz = z_sb[:, TPB * b:TPB * b + TPB, :]
                    link(nc.gpsimd.tensor_tensor(zz, zz, gab.unsqueeze(1).broadcast_to([P, TPB, D]), ALU.mult))
                    nc.gpsimd.tensor_tensor(zz, zz, beb.unsqueeze(1).broadcast_to([P, TPB, D]), ALU.add)\
                        .then_inc(g_z, 1)
            if STAGE >= 4:
                for i in range(SLOTS // P):
                    pool.dma_start(buf_d[i * P:(i + 1) * P, :], zero).then_inc(d_zero, 16)

            if STAGE < 2:
                return

            def set_low(u):
                pool.wait_ge(a_set, u + 1)
                _, src, dst = unit(u)
                nc.gpsimd.tensor_tensor(dst[1], src, dst[0], ALU.subtract).then_inc(g_set, 1)

            if STAGE >= 3:
                for u in range(KB // 2):
                    set_low(u)
            pool.wait_ge(s_stat, 2)
            inv_std(0, NT, s_rstd, mv, vareps, rstd, 1e-5)
            if STAGE >= 3:
                for u in range(KB // 2, KB):
                    set_low(u)
            if STAGE < 3:
                return
            pool.wait_ge(s_stat, 3)
            inv_std(0, NT, s_rstd, mv, vareps, rstd, 1e-5)
            pool.wait_ge(d_t, 32)
            for c in range(NGB * QT):
                pool.wait_ge(a_raw, c + 1)
                if c >= 2:
                    pool.wait_ge(g_rope, c - 1)
                r = raw[:, c % 2, :].rearrange("p (h s) -> p h s", h=2)
                sn = sinq[:, c % QT, :].rearrange("p (h s) -> p h s", h=2)
                o = t2[:, c % 2, :].rearrange("p (h s) -> p h s", h=2)
                nc.gpsimd.tensor_tensor(o[:, 0, :], r[:, 1, :], sn[:, 0, :], ALU.mult).then_inc(g_t2, 1)
                nc.gpsimd.tensor_tensor(o[:, 1, :], r[:, 0, :], sn[:, 1, :], ALU.mult).then_inc(g_t2, 1)
                pool.wait_ge(g_t2, 2 * c + 2)
                pool.wait_ge(v_t1, c + 1)
                if c >= QT:
                    pool.wait_ge(p_qz, c // QT)
                nc.gpsimd.tensor_tensor(rope[:, c % QT, :], t1[:, c % 2, :], t2[:, c % 2, :], ALU.add)\
                    .then_inc(g_rope, 1)
            if STAGE < 4:
                return
            pool.wait_ge(s_stat, 4)
            inv_std(0, NT, s_rstd, mv, vareps, rstd, 1e-5)
            for t in range(NT):
                pool.wait_ge(v_y3, t + 1)
                if t == 0:
                    pool.wait_ge(p_out, NGB)
                link(nc.gpsimd.tensor_copy(rows[:, t, 0:D], y_sb[:, t, :]))
                nc.gpsimd.tensor_tensor(rows[:, t, D:2 * D], y_sb[:, t, :], rows[:, t, 0:D], ALU.subtract)\
                    .then_inc(g_row, 1)
            pool.wait_ge(v_idx, 1)
            pool.wait_ge(g_row, NT)
            for i in range(NT * TOPK):
                nc.gpsimd.indirect_dma_start(
                    out=buf_d[:, :], out_offset=bass.IndirectOffsetOnAxis(ap=scat[:, i:i + 1], axis=0),
                    in_=rows[:, i // TOPK, :], in_offset=None).then_inc(d_scat, 16)
            for e in range(NE):
                for m in range(MH):
                    n = e * MH + m
                    pool.wait_ge(v_h, n + 1)
                    nc.gpsimd.tensor_tensor(hs[1][:, m, :], hr[:, n % 2, :], hs[0][:, m, :], ALU.subtract)\
                        .then_inc(g_h, 1)
            pool.wait_ge(v_we, 4 * NE)
            pool.wait_ge(a_we, 4 * NE)
            for r in range(6):
                pool.wait_ge(d_oe[r], 16 * NE // 2)
            for i in range(NT * TOPK):
                nc.gpsimd.indirect_dma_start(
                    out=got[:, i // TOPK, (i % TOPK) * D:(i % TOPK + 1) * D], out_offset=None,
                    in_=oe_d[:, :], in_offset=bass.IndirectOffsetOnAxis(ap=gidx[:, i:i + 1], axis=0))\
                    .then_inc(d_got[i // TOPK], 16)

        @block.scalar
        def _(act):
            A_ = nc.scalar.activation
            act.dma_start(ctxT[0:DC, :], A["ctxT"]).then_inc(d_k, 16)
            act.dma_start(wkT[0:DC, :], A["W_kT"]).then_inc(d_k, 16)
            act.dma_start(bkc[0:DC, :], A["b_k"].rearrange("(p a) -> p a", a=1)).then_inc(d_k, 16)
            act.dma_start(gab, A["ln_gamma"].partition_broadcast(P)).then_inc(d_k, 16)
            act.dma_start(beb, A["ln_beta"].partition_broadcast(P)).then_inc(d_k, 16)
            act.dma_start(bkb, A["b_k"].partition_broadcast(P)).then_inc(d_k, 16)
            act.dma_start(identf[:, :], A["identf"]).then_inc(d_c, 16)
            act.dma_start(ident16[:, :], A["ident16"]).then_inc(d_c, 16)
            act.dma_start(identb[:, :], A["identb"]).then_inc(d_c, 16)
            act.dma_start(gx[:, :], A["g_xattn"].partition_broadcast(P)).then_inc(d_c, 16)
            act.dma_start(gf[:, :], A["g_ffn"].partition_broadcast(P)).then_inc(d_c, 16)
            act.dma_start(ctx_n[:, :, :], A["ctx"].rearrange("(t p) d -> p t d", p=P)).then_inc(d_c, 16)
            act.dma_start(kcos[:, :, :], A["kcos"]).then_inc(d_c, 16)
            act.dma_start(ksin[:, :, :], A["ksin"]).then_inc(d_c, 16)
            if STAGE >= 4:
                act.dma_start(b1s[:, :], A["b1T"]).then_inc(d_c, 16)
                act.dma_start(gwt[:, :, :], A["gating_w"].rearrange("(a p) n -> p a n", p=P)).then_inc(d_c, 16)
                act.dma_start(trib[:, :], A["trib"]).then_inc(d_c, 16)
                act.dma_start(iota8[:, :], A["iota8"]).then_inc(d_c, 16)
                act.dma_start(spare[:, :], A["spare"]).then_inc(d_c, 16)
            NC_ = 16 * (13 if STAGE >= 4 else 8)
            act.wait_ge(d_c, NC_)
            act.wait_ge(s_init, 5)
            act.wait_ge(d_k, 16 * 6)
            A_(tgx[:, :], gx[:, :], ACT.Tanh).then_inc(s_tanh, 1)
            A_(tgf[:, :], gf[:, :], ACT.Tanh).then_inc(s_tanh, 1)
            for i in range(2):
                act.wait_ge(p_kvT, i + 1)
                A_(kvT0[0:DC, 512 * i:512 * i + 512], bank[i][0:DC, :], ACT.Identity, bias=bkc[0:DC, :])\
                    .then_inc(a_kvT, 1)
            for s in range(B + 3):
                if s < B:
                    act.wait_ge(p_yT0, s + 1)
                    A_(yt_f[:, :, s * S:(s + 1) * S], bank[4 + s % 2][:, :].rearrange("p (a b) -> p a b", a=KC),
                       ACT.Copy).then_inc(a_yT0, 1)
                if 1 <= s <= B:
                    b = s - 1
                    act.wait_ge(p_oT, b + 1)
                    A_(outT[0:DC, b * S:(b + 1) * S], bank[6 + b % 2][0:DC, 0:S], ACT.Copy, scale=1 / 16.0)\
                        .then_inc(a_oT, 1)
                if s in (1, 2, 3):
                    i = s - 1
                    act.wait_ge(d_w, 16 * (i + 1))
                    A_((gtern, vtern, otern)[i].rearrange("p a b -> p (a b)"), wraw[i], ACT.Abs, accum_out=wabs[:, i:i + 1]).then_inc(a_abs, 1)
                if s >= 3:
                    b = s - 3
                    act.wait_ge(v_nm0, b + 1)
                    for t in (TPB * b, TPB * b + 1):
                        A_(z_sb[:, t, :], z_sb[:, t, :], ACT.Exp, bias=nm0[:, t:t + 1], accum_out=sum0[:, t:t + 1])\
                            .then_inc(a_exp0, 1)
            if STAGE < 2:
                return

            if STAGE >= 3:
                for u in range(KB):
                    act.wait_ge(p_set, u + 1)
                    src, st, dst = unit(u)
                    if u >= 2:
                        act.wait_ge(g_set, u - 1)
                    A_(st, src, ACT.Copy, scale=WS).then_inc(a_raws, 1)
                    A_(dst[0], src, ACT.Copy, scale=WS).then_inc(a_set, 1)

            def key_side(u):
                act.wait_ge(p_set, KB + u + 1)
                A_(zp[:, 4 * u:4 * u + 4, :], bank[7][:, :].rearrange("p (a b) -> p a b", a=4), ACT.Copy)\
                    .then_inc(a_set, 1)

            for s in range(NT + 2):
                for t in ([0, 1] if s == 0 else [s + 1] if s + 1 < NT else []):
                    act.wait_ge(p_qT, t + 1)
                    if t >= 2:
                        act.wait_ge(p_gv, t - 1)
                    A_(qT[:, t % 2, :], bank[0][:, 0:P].bitcast(BF16), ACT.Copy).then_inc(a_qT, 1)
                if s < NT:
                    act.wait_ge(v_gv, s + 1)
                    A_(g_sb[:, s % 2, :], g_sb[:, s % 2, :], ACT.Silu).then_inc(a_silu, 1)
                if STAGE >= 3 and s < NT:
                    key_side(s)
                if s >= 2:
                    act.wait_ge(p_hT, s - 1)
                    A_(hqT[:, s % 2, :], bank[5][:, :].bitcast(BF16), ACT.Copy).then_inc(a_hT, 1)
                if 1 <= s <= NT:
                    t = s - 1
                    act.wait_ge(v_qs2, t + 1)
                    A_(v_sb[:, t % 2, :], v_sb[:, t % 2, :], ACT.Identity, bias=magic[:, :], scale=qs2[:, t:t + 1])\
                        .then_inc(a_rnd, 1)
            if STAGE < 3:
                return
            if STAGE >= 4:
                act.wait_ge(d_zero, 16 * (SLOTS // P))
            for b in range(B):
                act.wait_ge(p_yT2, b + 1)
                A_(yth[:, :, b * S:(b + 1) * S], bank[b % 2][:, :].rearrange("p (a b) -> p a b", a=KC), ACT.Copy)\
                    .then_inc(a_yT2, 1)
            act.wait_ge(v_kr, 2)
            A_(kvr[0], kvdup[:, :, 0, :], ACT.Copy).then_inc(a_kr, 1)
            for i in range(2):
                act.wait_ge(p_kr, i + 1)
                A_(kvt[0][:, 512 * i:512 * i + 512], bank[2 + i][:, :], ACT.Copy).then_inc(a_kr, 1)

            def raw_copy(c):
                act.wait_ge(p_qb, c + 1)
                if c == 0:
                    act.wait_ge(v_krl, 1)
                if c >= 2:
                    act.wait_ge(g_t2, 2 * (c - 1))
                A_(raw[:, c % 2, :], bank[c % 2][:, :], ACT.Copy).then_inc(a_raw, 1)

            def qz_high(g):
                act.wait_ge(p_qz, g + 1)
                if g >= 2:
                    act.wait_ge(p_sc, G * (g - 1))
                A_(qz[0][:, g % 2, :], bank[2][:, :], ACT.Copy).then_inc(a_qz, 1)

            def exps(n):
                g, h = n // G, n % G
                act.wait_ge(v_max, n + 1)
                if n >= 2:
                    act.wait_ge(p_at, n - 1)
                if h == 0 and g >= 2:
                    act.wait_ge(v_norm, g - 1)
                for st in range(TPB):
                    A_(e_sb[:, n % 2, st * S:(st + 1) * S], bank[3 + n % 2][:, st * S:(st + 1) * S], ACT.Exp,
                       bias=nmax[:, n % 2, st:st + 1], accum_out=esum[:, g % 2, st, h:h + 1]).then_inc(a_exp, 1)

            def at_high(n):
                act.wait_ge(p_at, n + 1)
                if n >= 2:
                    act.wait_ge(p_cx, n - 1)
                A_(at[0][:, n % 2, :], bank[5][:, :], ACT.Copy).then_inc(a_at, 1)

            def ct_high(g):
                act.wait_ge(p_ct, g + 1)
                if g >= 1:
                    act.wait_ge(p_out, g)
                A_(ct[0], bank[2][:, :], ACT.Copy).then_inc(a_ct, 1)

            def split_high(k):
                e, q = k // 4, k % 4
                act.wait_ge(d_e, 32 * (e + 1))
                if e >= 2:
                    act.wait_ge(p_oe, 3 * (e - 1))
                A_(we[q // 2][0][:, e % 2, (q % 2) * EH:(q % 2 + 1) * EH],
                   eraw[:, q // 2, (q % 2) * EH:(q % 2 + 1) * EH], ACT.Copy, scale=WS).then_inc(a_we, 1)

            for g in range(2):
                for c in range(QT * g, QT * g + QT):
                    raw_copy(c)
                if g == 0:
                    qz_high(0)
            exps(0)
            for n in range(NHB):
                g, h = n // G, n % G
                at_high(n)
                if n + 1 < NHB:
                    exps(n + 1)
                for c in tiles_at(n):
                    raw_copy(c)
                if h == 1 and g + 1 < NGB:
                    qz_high(g + 1)
                if h == 2 and g >= 1:
                    ct_high(g - 1)
                if STAGE >= 4 and n in (24, 28, 32, 36):
                    split_high((n - 24) // 4)
            ct_high(NGB - 1)
            if STAGE < 4:
                return
            for s in range(NT // 2):
                act.wait_ge(p_yT3, s + 1)
                A_(yt_f[:, :, s * S:(s + 1) * S], bank[s % 2][:, :].rearrange("p (a b) -> p a b", a=KC), ACT.Copy)\
                    .then_inc(a_yT3, 1)
            act.wait_ge(v_el, 1)
            A_(el[:, :, :], el[:, :, :], ACT.Exp).then_inc(a_el, 1)

            def rows_high(e):
                act.wait_ge(p_bT, 2 * e + 1)
                if e >= 1:
                    act.wait_ge(p_h, MH * e)
                A_(bufT[:, 0, :], bank[0][:, :].bitcast(F16)[:, 0:KC * CAP], ACT.Copy).then_inc(a_bT, 1)

            rows_high(0)
            for e in range(NE):
                for m in range(MH):
                    n = e * MH + m
                    act.wait_ge(p_h, n + 1)
                    if m == 0 and e >= 1:
                        act.wait_ge(p_oe, 3 * e)
                    A_(hs[0][:, m, :], bank[2 + n % 3][:, 0:CAP], ACT.Relu, bias=b1w[:, n:n + 1]).then_inc(a_h, 1)
                if e + 1 < NE:
                    rows_high(e + 1)
                    for q in range(4):
                        split_high(4 * (e + 1) + q)

        @block.vector
        def _(dve):
            V = nc.vector
            chain = [0]

            def link(ins):
                chain[0] += 1
                ins.then_inc(c_dve, 1)
                dve.wait_ge(c_dve, chain[0])

            def normed(t, sig):
                V.tensor_scalar(y_sb[:, t, :], x_sb[:, t, :], mv[:, t, 0:1], rstd[:, t:t + 1],
                                ALU.subtract, ALU.mult).then_inc(sig, 1)

            def all_stats(k):
                for t in range(NT):
                    ins = V.bn_stats(stats[:, t, :], x_sb[:, t, :])
                link(ins)
                for t in range(NT):
                    ins = V.bn_aggr(mv[:, t, :], stats[:, t, :])
                ins.then_inc(s_stat, 1)
                dve.wait_ge(s_rstd, k)

            dve.wait_ge(d_x, 32)
            all_stats(1)
            for t in range(NT):
                normed(t, v_y0)
            dve.wait_ge(p_kv, 1)
            dve.wait_ge(d_k, 96)
            V.tensor_tensor(kv0, bank[2][:, :].rearrange("p (a b) -> p a b", a=NT),
                            bkb.unsqueeze(1).broadcast_to([P, NT, DC]), ALU.add).then_inc(v_kv, 1)

            def ternary(i, dst):
                if i == 0:
                    dve.wait_ge(p_abs, 1)
                    link(V.tensor_scalar(gw[:, :], bank[3][:, 0:3], 1.0 / (FH * D), 1e-5, ALU.mult, ALU.max))
                    V.tensor_scalar(thr[:, :], gw[:, :], 0.5, None, ALU.mult)
                    link(V.tensor_scalar(nthr[:, :], gw[:, :], -0.5, None, ALU.mult))
                link(V.tensor_scalar(dst, wraw[i], nthr[:, i:i + 1], None, ALU.is_lt))
                V.scalar_tensor_tensor(dst, wraw[i], thr[:, i:i + 1], dst, ALU.is_gt, ALU.subtract)\
                    .then_inc(v_tern, 1)

            for s in range(B + 3):
                if s < B:
                    dve.wait_ge(p_sim, s + 1)
                    sm = bank[s % 2][:, :].rearrange("p (a b) -> p a b", a=TPB)
                    for i in range(TPB):
                        ins = V.bn_stats(stats2[:, TPB * s + i, :], sm[:, i, :])
                    link(ins)
                    for i in range(TPB):
                        ins = V.bn_aggr(mv2[:, TPB * s + i, :], stats2[:, TPB * s + i, :])
                    ins.then_inc(v_sst, 1)
                    dve.wait_ge(g_srs, s + 1)
                    for i in range(TPB):
                        t = TPB * s + i
                        ins = V.tensor_scalar(z_sb[:, t, :], sm[:, i, :], mv2[:, t, 0:1], rstd2[:, t:t + 1],
                                              ALU.subtract, ALU.mult)
                    ins.then_inc(v_z, 1)
                if 1 <= s <= B:
                    b = s - 1
                    dve.wait_ge(g_z, b + 1)
                    V.tensor_reduce(nm0[:, TPB * b:TPB * b + TPB], z_sb[:, TPB * b:TPB * b + TPB, :], AX.X, ALU.max,
                                    negate=True).then_inc(v_nm0, 1)
                if s >= B and STAGE >= 2:
                    ternary(s - B, (gtern, vtern, otern)[s - B].rearrange("p a b -> p (a b)"))
                if s >= 3:
                    b = s - 3
                    dve.wait_ge(a_exp0, TPB * (b + 1))
                    if b == 0:
                        dve.wait_ge(s_tanh, 2)
                    ts = slice(TPB * b, TPB * b + TPB)
                    link(V.reciprocal(r0[:, ts], sum0[:, ts]))
                    link(V.tensor_scalar(r0[:, ts], r0[:, ts], tgx[:, 0:1], None, ALU.mult))
                    for t in (TPB * b, TPB * b + 1):
                        V.scalar_tensor_tensor(x_sb[:, t, :], z_sb[:, t, :], r0[:, t:t + 1], x_sb[:, t, :],
                                               ALU.mult, ALU.add).then_inc(s_upd, 1)
            if STAGE < 2:
                for t in range(NT):
                    dve.wait_ge(s_upd, NT)
                    V.tensor_copy(y_sb[:, t, :], x_sb[:, t, :]).then_inc(v_fin, 1)
                return
            dve.wait_ge(s_upd, NT)
            all_stats(2)
            for t in range(NT):
                ins = V.tensor_scalar(y_sb[:, t, :], x_sb[:, t, :], mv[:, t, 0:1], rstd[:, t:t + 1],
                                      ALU.subtract, ALU.mult)
            link(ins)
            link(V.tensor_reduce(am[:, :], y_sb[:, :, :], AX.X, ALU.max, apply_absolute_value=True))
            link(V.tensor_scalar(am[:, :], am[:, :], 1e-5, None, ALU.max))
            link(V.reciprocal(qs[:, :], am[:, :]))
            link(V.tensor_scalar(qs[:, :], qs[:, :], 127.0, None, ALU.mult))
            V.tensor_scalar(sgs[:, :], am[:, :], gw[:, 0:1], 1 / 127.0, ALU.mult, ALU.mult)
            V.tensor_scalar(svs[:, :], am[:, :], gw[:, 1:2], 1 / 127.0, ALU.mult, ALU.mult)
            for t in range(NT):
                ins = V.tensor_scalar(y_sb[:, t, :], y_sb[:, t, :], qs[:, t:t + 1], MAGIC, ALU.mult, ALU.add)
            link(ins)
            for t in range(NT):
                V.tensor_scalar(q_sb[:, t, :], y_sb[:, t, :], MAGIC, 127.0, ALU.subtract, ALU.min).then_inc(v_q, 1)
            dve.wait_ge(d_gb, 48)

            for s in range(NT + 2):
                if s < NT:
                    dve.wait_ge(p_gv, s + 1)
                    if s >= 2:
                        dve.wait_ge(v_hq, s - 1)
                    for i in range(2):
                        V.scalar_tensor_tensor(v_sb[:, s % 2, 512 * i:512 * i + 512], bank[3 + i][:, :], svs[:, s:s + 1],
                                               vb_b[:, 512 * i:512 * i + 512], ALU.mult, ALU.add)
                    for i in range(2):
                        ins = V.scalar_tensor_tensor(g_sb[:, s % 2, 512 * i:512 * i + 512], bank[1 + i][:, :],
                                                     sgs[:, s:s + 1], gb_b[:, 512 * i:512 * i + 512],
                                                     ALU.mult, ALU.add)
                    ins.then_inc(v_gv, 1)
                if 1 <= s <= NT:
                    t, r = s - 1, (s - 1) % 2
                    dve.wait_ge(a_silu, t + 1)
                    dve.wait_ge(v_gv, t + 1)
                    link(V.tensor_tensor(v_sb[:, r, :], v_sb[:, r, :], g_sb[:, r, :], ALU.mult))
                    link(V.tensor_reduce(am2[:, t:t + 1], v_sb[:, r, :], AX.X, ALU.max, apply_absolute_value=True))
                    link(V.tensor_scalar(am2[:, t:t + 1], am2[:, t:t + 1], 1e-5, None, ALU.max))
                    link(V.reciprocal(qs2[:, t:t + 1], am2[:, t:t + 1]))
                    V.tensor_scalar(qs2[:, t:t + 1], qs2[:, t:t + 1], 127.0, None, ALU.mult).then_inc(v_qs2, 1)
                    V.tensor_scalar(sos[:, t:t + 1], am2[:, t:t + 1], gw[:, 2:3], 1 / 127.0, ALU.mult, ALU.mult)
                if s >= 2:
                    t = s - 2
                    dve.wait_ge(p_fo, t + 1)
                    dve.wait_ge(s_upd, NT + t)
                    V.scalar_tensor_tensor(fo, bank[6][:, 0:D], sos[:, t:t + 1], ob_b, ALU.mult, ALU.add)\
                        .then_inc(v_fo, 1)
                    dve.wait_ge(v_fo, t + 1)
                    V.scalar_tensor_tensor(x_sb[:, t, :], fo, tgf[:, 0:1], x_sb[:, t, :], ALU.mult, ALU.add)\
                        .then_inc(s_upd, 1)
                if 1 <= s <= NT:
                    t, r = s - 1, (s - 1) % 2
                    dve.wait_ge(a_rnd, t + 1)
                    if t >= 2:
                        dve.wait_ge(p_hT, t - 1)
                    V.tensor_scalar(hq[:, r, :], v_sb[:, r, :], MAGIC, 127.0, ALU.subtract, ALU.min).then_inc(v_hq, 1)
            if STAGE < 3:
                for t in range(NT):
                    dve.wait_ge(s_upd, 2 * NT)
                    V.tensor_copy(y_sb[:, t, :], x_sb[:, t, :]).then_inc(v_fin, 1)
                return
            kt = kvdup
            xr = ctx_n[:, :, :].rearrange("p (b i) d -> p b i d", b=B)
            yb = y_sb[:, 0:2, :].rearrange("p a b -> p (a b)")
            ya = yb.rearrange("p (b i d) -> p b i d", b=B, i=TPB)
            for b in range(B):
                V.tensor_tensor(ya[:, b, :, 0:DC // 2], xr[:, b, :, DC // 2:DC], ksin[:, :, 0:DC // 2], ALU.mult)
                ins = V.tensor_tensor(ya[:, b, :, DC // 2:DC], xr[:, b, :, 0:DC // 2], ksin[:, :, DC // 2:DC], ALU.mult)
            link(ins)
            for b in range(B):
                ins = V.tensor_tensor(xr[:, b], xr[:, b], kcos[:, :, :], ALU.mult)
            link(ins)
            dve.wait_ge(a_hT, NT)
            dve.wait_ge(p_fo, NT)
            for j in range(2):
                V.tensor_tensor(kt[:, :, j, :], ctx_n[:, :, :], yb.rearrange("p (t d) -> p t d", t=NT), ALU.add)\
                    .then_inc(v_kr, 1)
            dve.wait_ge(s_upd, 2 * NT)
            all_stats(3)
            for t in range(NT):
                normed(t, v_y2)
            for b in range(B):
                dve.wait_ge(a_yT2, b + 1)
                V.tensor_tensor(ytl[:, :, b * S:(b + 1) * S], bank[b % 2][:, :].rearrange("p (a b) -> p a b", a=KC),
                                yth[:, :, b * S:(b + 1) * S], ALU.subtract).then_inc(v_yT2, 1)
            dve.wait_ge(a_kr, 1)
            V.tensor_tensor(kvr[1], kt[:, :, 0, :], kvr[0], ALU.subtract).then_inc(v_krl, 1)
            for i in range(2):
                dve.wait_ge(a_kr, i + 2)
                V.tensor_tensor(kvt[1][:, 512 * i:512 * i + 512], bank[2 + i][:, :],
                                kvt[0][:, 512 * i:512 * i + 512], ALU.subtract).then_inc(v_krl, 1)
            V.tensor_scalar(tgx1[:, :], tgx[:, 1:2], 1.0 / WS, None, ALU.mult)
            dve.wait_ge(d_t, 32)

            def turn(c):
                dve.wait_ge(a_raw, c + 1)
                if c >= 2:
                    dve.wait_ge(g_rope, c - 1)
                V.tensor_tensor(t1[:, c % 2, :], bank[c % 2][:, :], cosq[:, c % QT, :], ALU.mult).then_inc(v_t1, 1)

            def qz_low(g):
                dve.wait_ge(a_qz, g + 1)
                V.tensor_tensor(qz[1][:, g % 2, :], bank[2][:, :], qz[0][:, g % 2, :], ALU.subtract).then_inc(v_qz, 1)

            def maxima(n):
                dve.wait_ge(p_sc, n + 1)
                if n >= 2:
                    dve.wait_ge(a_exp, TPB * (n - 1))
                V.tensor_reduce(nmax[:, n % 2, :], bank[3 + n % 2][:, :].rearrange("p (a b) -> p a b", a=TPB),
                                AX.X, ALU.max, negate=True).then_inc(v_max, 1)

            def at_low(n):
                dve.wait_ge(a_at, n + 1)
                V.tensor_tensor(at[1][:, n % 2, :], bank[5][:, :], at[0][:, n % 2, :], ALU.subtract).then_inc(v_at, 1)

            def norm(g):
                dve.wait_ge(a_exp, TPB * G * (g + 1))
                rs = rsum[:, g % 2].rearrange("p a b -> p (a b)")
                link(V.reciprocal(rs, esum[:, g % 2].rearrange("p a b -> p (a b)")))
                dve.wait_ge(p_cx, G * (g + 1))
                if g >= 1:
                    dve.wait_ge(p_ct, g)
                V.tensor_tensor(cxn.rearrange("p (a b) -> p a b", b=DC),
                                bank[6][:, :].rearrange("p (a b) -> p a b", b=DC),
                                rs.unsqueeze(2).broadcast_to([P, TPB * G, DC]), ALU.mult).then_inc(v_norm, 1)

            def ct_low(g):
                dve.wait_ge(a_ct, g + 1)
                V.tensor_tensor(ct[1], bank[2][:, :], ct[0], ALU.subtract).then_inc(v_ct, 1)

            def update(b):
                dve.wait_ge(p_out, NG * (b + 1))
                ts = slice(TPB * b, TPB * b + TPB)
                V.scalar_tensor_tensor(x_sb[:, ts, :], bank[7][:, :].rearrange("p (a b) -> p a b", a=TPB), tgx1[:, 0:1],
                                       x_sb[:, ts, :], ALU.mult, ALU.add).then_inc(s_upd, 1)

            def split_low(k):
                e, q = k // 4, k % 4
                part = slice((q % 2) * EH, (q % 2 + 1) * EH)
                dve.wait_ge(a_we, k + 1)
                V.scalar_tensor_tensor(we[q // 2][1][:, e % 2, part], eraw[:, q // 2, part], WS,
                                       we[q // 2][0][:, e % 2, part], ALU.mult, ALU.subtract).then_inc(v_we, 1)

            for g in range(2):
                for c in range(QT * g, QT * g + QT):
                    turn(c)
                if g == 0:
                    qz_low(0)
            maxima(0)
            maxima(1)
            for n in range(NHB):
                g, h = n // G, n % G
                at_low(n)
                if h == 0 and g >= 1:
                    norm(g - 1)
                if n + 2 < NHB:
                    maxima(n + 2)
                for c in tiles_at(n):
                    turn(c)
                if h == 1 and g + 1 < NGB:
                    qz_low(g + 1)
                if h == 2 and g >= 1:
                    ct_low(g - 1)
                if h == 3 and g >= 1 and g % NG == 0:
                    update(g // NG - 1)
                if STAGE >= 4 and n in (24, 28, 32, 36):
                    split_low((n - 24) // 4)
            norm(NGB - 1)
            ct_low(NGB - 1)
            update(B - 1)
            if STAGE < 4:
                for t in range(NT):
                    dve.wait_ge(s_upd, 2 * NT + B)
                    V.tensor_copy(y_sb[:, t, :], x_sb[:, t, :]).then_inc(v_fin, 1)
                return
            V.tensor_scalar(b1w[:, :], b1s[:, :], WS, None, ALU.mult)
            dve.wait_ge(s_upd, 2 * NT + B)
            all_stats(4)
            for t in range(NT):
                normed(t, v_y3)
            dve.wait_ge(p_lg, 1)
            lg = bank[2][:, 0:NT * NE].rearrange("p (a b) -> p a b", a=NT)
            link(V.tensor_reduce(mx[:, :], lg, AX.X, ALU.max))
            V.tensor_tensor(el[:, :, :], lg, mx[:, :].unsqueeze(2).broadcast_to([P, NT, NE]), ALU.subtract)\
                .then_inc(v_el, 1)
            dve.wait_ge(a_el, 1)
            link(V.tensor_reduce(es[:, :], el[:, :, :], AX.X, ALU.add))
            link(V.reciprocal(es[:, :], es[:, :]))
            link(V.tensor_tensor(gates[:, :, :], el[:, :, :], es[:, :].unsqueeze(2).broadcast_to([P, NT, NE]), ALU.mult))
            for t in range(NT):
                ins = V.max(v8[:, t, :], gates[:, t, :])
            link(ins)
            for t in range(NT):
                ins = V.max_index(i8[:, t, :], v8[:, t, :], gates[:, t, :])
            link(ins)
            link(V.tensor_copy(idf[:, :, :], i8[:, :, 0:TOPK]))
            for k in range(TOPK):
                ins = V.tensor_tensor(oh[:, :, k, :], iota8[:, :].unsqueeze(1).broadcast_to([P, NT, NE]),
                                      idf[:, :, k].unsqueeze(2).broadcast_to([P, NT, NE]), ALU.is_equal)
            link(ins)
            V.tensor_tensor(ohs[:, :, :], oh[:, :, 0, :], oh[:, :, 1, :], ALU.add).then_inc(v_oh, 1)
            dve.wait_ge(p_pos, 1)
            cnt = bank[3][:, 0:NT * NE].rearrange("p (a b) -> p a b", a=NT)
            for k in range(TOPK):
                ins = V.tensor_tensor(pr[:, :, k, :], cnt, oh[:, :, k, :], ALU.mult)
            link(ins)
            link(V.tensor_reduce(pos[:, :, :], pr[:, :, :, :], AX.X, ALU.add))
            V.tensor_scalar(val[:, :, :], pos[:, :, :], float(CAP), None, ALU.is_lt)
            link(V.tensor_scalar(base[:, :, :], idf[:, :, :], float(CAP), None, ALU.mult))
            link(V.tensor_tensor(sl[:, :, :], pos[:, :, :], base[:, :, :], ALU.add))
            link(V.scalar_tensor_tensor(sl2[:, :, :], sl[:, :, :], spare[:, 0:1], val[:, :, :], ALU.subtract, ALU.mult))
            V.tensor_scalar(scat[:, :], sl2[:, :, :].rearrange("p a b -> p (a b)"), spare[:, 0:1], None, ALU.add)
            link(V.scalar_tensor_tensor(gi[:, :, :], pos[:, :, :], float(CAP - 1), base[:, :, :], ALU.min, ALU.add))
            V.tensor_copy(gidx[:, :], gi[:, :, :].rearrange("p a b -> p (a b)")).then_inc(v_idx, 1)
            link(V.tensor_tensor(ws[:, :], v8[:, :, 0], v8[:, :, 1], ALU.add))
            link(V.tensor_scalar(ws[:, :], ws[:, :], 1e-8, None, ALU.add))
            link(V.reciprocal(ws[:, :], ws[:, :]))
            link(V.tensor_tensor(wn[:, :, :], v8[:, :, 0:TOPK], ws[:, :].unsqueeze(2).broadcast_to([P, NT, TOPK]), ALU.mult))
            link(V.tensor_tensor(wn[:, :, :], wn[:, :, :], val[:, :, :], ALU.mult))
            link(V.tensor_scalar(wn[:, :, :], wn[:, :, :], tgf[:, 1:2], None, ALU.mult))
            dve.wait_ge(d_b, 16)

            def rows_low(e):
                dve.wait_ge(p_bT, 2 * e + 2)
                if e >= 1:
                    dve.wait_ge(p_h, MH * e)
                V.tensor_copy(bufT[:, 1, :], bank[1][:, :].bitcast(F16)[:, 0:KC * CAP]).then_inc(v_bT, 1)

            rows_low(0)
            for e in range(NE):
                for m in range(MH):
                    n = e * MH + m
                    dve.wait_ge(a_h, n + 1)
                    if n >= 2:
                        dve.wait_ge(g_h, n - 1)
                    V.tensor_scalar(hr[:, n % 2, :], bank[2 + n % 3][:, 0:CAP], b1w[:, n:n + 1], 0.0, ALU.add, ALU.max)\
                        .then_inc(v_h, 1)
                if e + 1 < NE:
                    rows_low(e + 1)
                    for q in range(4):
                        split_low(4 * (e + 1) + q)
                for i in range(3):
                    k = 3 * e + i
                    w = min(P, CAP - P * i)
                    dve.wait_ge(p_oe, k + 1)
                    if k >= 6:
                        dve.wait_ge(d_oe[k % 6], 16 * (k // 6))
                    V.scalar_tensor_tensor(oe[0:w, k % 6, :], bank[5 + i][0:w, 0:D], 1.0 / (WS * WS), b2b[0:w, e, :],
                                           ALU.mult, ALU.add).then_inc(v_oe, 1)
            for t in range(NT):
                dve.wait_ge(d_got[t], 16 * TOPK)
                link(V.scalar_tensor_tensor(x_sb[:, t, :], got[:, t, 0:D], wn[:, t, 0:1], x_sb[:, t, :],
                                            ALU.mult, ALU.add))
                V.scalar_tensor_tensor(x_sb[:, t, :], got[:, t, D:2 * D], wn[:, t, 1:2], x_sb[:, t, :],
                                       ALU.mult, ALU.add).then_inc(v_fin, 1)

        @block.tensor
        def _(pe):
            M = nc.tensor.matmul
            TR = nc.tensor.transpose
            pe.wait_ge(d_k, 96)
            for i in range(2):
                M(bank[i][0:DC, :], wkT[0:DC, :], ctxT[0:DC, 512 * i:512 * i + 512], start=True, stop=True)\
                    .then_inc(p_kvT, 1)
            for t in range(NT):
                ins = M(bank[2][:, t * DC:(t + 1) * DC], ctxT[0:DC, t * P:(t + 1) * P], wkT[0:DC, :],
                        start=True, stop=True)
            ins.then_inc(p_kv, 1)
            pe.wait_ge(d_c, 16)
            pe.wait_ge(d_c, 16 * (13 if STAGE >= 4 else 8))
            for s in range(B + 1):
                if s < B:
                    pe.wait_ge(v_y0, TPB * (s + 1))
                    if s >= 2:
                        pe.wait_ge(a_yT0, s - 1)
                    for it in range(TPB):
                        for jc in range(KC):
                            ins = TR(bank[4 + s % 2][:, jc * S + it * P:jc * S + (it + 1) * P],
                                     y_sb[:, TPB * s + it, jc * P:(jc + 1) * P], identf[:, :])
                    ins.then_inc(p_yT0, 1)
                if s >= 1:
                    b = s - 1
                    pe.wait_ge(a_yT0, b + 1)
                    if b == 0:
                        pe.wait_ge(v_kv, 1)
                    if b >= 2:
                        pe.wait_ge(a_oT, b - 1)
                    for jc in range(KC):
                        ins = M(bank[6 + b % 2][0:DC, 0:S], kv0[:, TPB * b + jc, :], yt_f[:, jc, b * S:(b + 1) * S],
                                start=(jc == 0), stop=(jc == KC - 1))
                    ins.then_inc(p_oT, 1)
                    pe.wait_ge(a_oT, b + 1)
                    if b == 0:
                        pe.wait_ge(a_kvT, 2)
                    if b >= 2:
                        pe.wait_ge(v_z, b - 1)
                    for it in range(TPB):
                        t = TPB * b + it
                        ins = M(bank[b % 2][:, it * S:(it + 1) * S], outT[0:DC, t * P:(t + 1) * P],
                                kvT0[0:DC, b * S:(b + 1) * S], start=True, stop=True)
                    ins.then_inc(p_sim, 1)
            if STAGE < 2:
                return
            pe.wait_ge(s_init, 5)
            pe.wait_ge(a_abs, 3)
            M(bank[3][:, 0:3], onesf[:, :], wabs[:, :], start=True, stop=True).then_inc(p_abs, 1)

            if STAGE >= 3:
                pe.wait_ge(a_oT, B)
                for u in range(KB):
                    if u >= 4:
                        pe.wait_ge(a_set, u - 3)
                    bk = bank[4 + u % 4]
                    if u < NH:
                        if u == 0:
                            pe.wait_ge(d_m, 32)
                        for kc in range(KC):
                            ins = M(bk[:, kc * DCQ:(kc + 1) * DCQ], wq[:, u, kc * P:(kc + 1) * P], kcq[:, u, :],
                                    start=True, stop=True)
                    else:
                        if u == NH:
                            pe.wait_ge(d_n, 32)
                        for i in range(2):
                            h = 2 * (u - NH) + i
                            ins = M(bk[i * DC:(i + 1) * DC, 0:D], kckv[:, h, :], woT[:, h, :], start=True, stop=True)
                    ins.then_inc(p_set, 1)

            def key_side(u):
                if u == 0:
                    pe.wait_ge(d_z, 32)
                pe.wait_ge(a_set, KB + u)
                for j in range(4):
                    k = 4 * u + j
                    ins = M(bank[7][:, j * P:(j + 1) * P], zl[:, k, :], zr[:, 2 * (k // 8) + j // 2, :],
                            start=True, stop=True)
                ins.then_inc(p_set, 1)

            def turn_q(t):
                pe.wait_ge(v_q, t + 1)
                if t >= 1:
                    pe.wait_ge(a_qT, t)
                for kc in range(KC):
                    ins = TR(bank[0][:, 0:P].bitcast(BF16)[:, kc * P:(kc + 1) * P], q_sb[:, t, kc * P:(kc + 1) * P],
                             identb[:, :])
                ins.then_inc(p_qT, 1)

            for s in range(NT + 2):
                if s == 0:
                    pe.wait_ge(v_z, B)
                    pe.wait_ge(a_oT, B)
                    if STAGE >= 3:
                        pe.wait_ge(a_set, KB)
                    turn_q(0)
                if s < NT:
                    pe.wait_ge(a_qT, s + 1)
                    if s == 0:
                        pe.wait_ge(v_tern, 3)
                    if s >= 1:
                        pe.wait_ge(v_gv, s)
                    for w, o in ((vtern, 3), (gtern, 1)):
                        for i in range(2):
                            for kc in range(KC):
                                ins = M(bank[o + i][:, :], qT[:, s % 2, kc * P:(kc + 1) * P],
                                        w[:, kc, 512 * i:512 * i + 512], start=(kc == 0), stop=(kc == KC - 1))
                    ins.then_inc(p_gv, 1)
                    if s + 1 < NT:
                        turn_q(s + 1)
                    if STAGE >= 3:
                        key_side(s)
                if s >= 2:
                    t = s - 2
                    pe.wait_ge(v_hq, t + 1)
                    if t >= 1:
                        pe.wait_ge(a_hT, t)
                    for j in range(FH // P):
                        ins = TR(bank[5][:, :].bitcast(BF16)[:, j * P:(j + 1) * P], hq[:, t % 2, j * P:(j + 1) * P],
                                 identb[:, :])
                    ins.then_inc(p_hT, 1)
                    pe.wait_ge(a_hT, t + 1)
                    if t >= 1:
                        pe.wait_ge(v_fo, t)
                    for j in range(FH // P):
                        ins = M(bank[6][:, 0:D], hqT[:, t % 2, j * P:(j + 1) * P], otern[:, j, :],
                                start=(j == 0), stop=(j == FH // P - 1))
                    ins.then_inc(p_fo, 1)
            if STAGE < 3:
                return
            for b in range(B):
                pe.wait_ge(v_y2, TPB * (b + 1))
                if b == 0:
                    pe.wait_ge(v_gv, NT)
                if b >= 2:
                    pe.wait_ge(v_yT2, b - 1)
                for it in range(TPB):
                    for kc in range(KC):
                        ins = TR(bank[b % 2][:, kc * S + it * P:kc * S + (it + 1) * P],
                                 y_sb[:, TPB * b + it, kc * P:(kc + 1) * P], identf[:, :])
                ins.then_inc(p_yT2, 1)
            pe.wait_ge(v_kr, 2)
            for i in range(2):
                for j in range(4):
                    ins = TR(bank[2 + i][:, j * P:(j + 1) * P], kvdup[:, 4 * i + j].rearrange("p a b -> p (a b)"),
                             identf[:, :])
                ins.then_inc(p_kr, 1)

            def queries(c):
                g, t = c // QT, c % QT
                b, col = g // NG, (g % NG) * G * HALF + t * P
                if c == 0:
                    pe.wait_ge(v_yT2, B)
                    pe.wait_ge(g_set, KB)
                if c >= 2:
                    pe.wait_ge(v_t1, c - 1)
                for half in range(2):
                    n = 0
                    for a, w in PASSES:
                        for kc in range(KC):
                            ins = M(bank[c % 2][:, half * S:(half + 1) * S], m1[w][:, kc, half, col:col + P],
                                    (yth, ytl)[a][:, kc, b * S:(b + 1) * S], start=(n == 0), stop=(n == 5))
                            n += 1
                ins.then_inc(p_qb, 1)

            def latent(g):
                pe.wait_ge(g_rope, QT * (g + 1))
                if g == 0:
                    pe.wait_ge(a_set, NSET)
                    pe.wait_ge(v_krl, 3)
                if g >= 1:
                    pe.wait_ge(v_qz, g)
                if g >= 3:
                    pe.wait_ge(v_ct, g - 2)
                for pair in range(2):
                    n = 0
                    for half in range(2):
                        for j in (2 * pair, 2 * pair + 1):
                            t = (j + 1) // 2
                            ins = M(bank[2][:, pair * S:(pair + 1) * S], zp[:, ((g % NG) * 2 + half) * 4 + j, :],
                                    rope[:, t, half * S:(half + 1) * S], start=(n == 0), stop=(n == 3))
                            n += 1
                ins.then_inc(p_qz, 1)

            def scores(n):
                g, h = n // G, n % G
                b, po, pair = n // NH, (h % 2) * DC, h // 2
                if h == 0:
                    pe.wait_ge(v_qz, g + 1)
                if n >= 2:
                    pe.wait_ge(a_exp, TPB * (n - 1))
                for st in range(TPB):
                    col = pair * S + st * P
                    for i, (a, w) in enumerate(PASSES):
                        ins = M(bank[3 + n % 2][:, st * S:(st + 1) * S], qz[a][po:po + DC, g % 2, col:col + P],
                                kvt[w][po:po + DC, b * S:(b + 1) * S], start=(i == 0), stop=(i == 2))
                ins.then_inc(p_sc, 1)

            def turn_scores(n):
                pe.wait_ge(a_exp, TPB * (n + 1))
                if n >= 1:
                    pe.wait_ge(v_at, n)
                for st in range(TPB):
                    for lt in range(TPB):
                        ins = TR(bank[5][:, lt * S + st * P:lt * S + (st + 1) * P],
                                 e_sb[:, n % 2, st * S + lt * P:st * S + (lt + 1) * P], identf[:, :])
                ins.then_inc(p_at, 1)

            def context(n):
                g, h, b = n // G, n % G, n // NH
                pe.wait_ge(v_at, n + 1)
                if h == 0 and g >= 1:
                    pe.wait_ge(v_norm, g)
                for st in range(TPB):
                    k = 0
                    for lt in range(TPB):
                        for a, w in PASSES:
                            ins = M(bank[6][:, st * S + h * DC:st * S + (h + 1) * DC],
                                    at[a][:, n % 2, lt * S + st * P:lt * S + (st + 1) * P],
                                    kvr[w][:, TPB * b + lt, :], start=(k == 0), stop=(k == 5))
                            k += 1
                ins.then_inc(p_cx, 1)

            def turn_context(g):
                pe.wait_ge(v_norm, g + 1)
                pe.wait_ge(v_qz, min(g + 3, NGB))
                for st in range(TPB):
                    for pair in range(2):
                        ins = TR(bank[2][:, pair * S + st * P:pair * S + (st + 1) * P],
                                 cxn[:, st * S + pair * P:st * S + (pair + 1) * P], identf[:, :])
                ins.then_inc(p_ct, 1)

            def project(g):
                b = g // NG
                pe.wait_ge(v_ct, g + 1)
                if g % NG == 0 and b >= 1:
                    pe.wait_ge(s_upd, 2 * NT + b)
                for pair in range(2):
                    for a, w in PASSES:
                        for st in range(TPB):
                            first = g % NG == 0 and pair == 0 and (a, w) == (0, 0)
                            last = g % NG == NG - 1 and pair == 1 and (a, w) == PASSES[-1]
                            ins = M(bank[7][:, st * S:(st + 1) * S], ct[a][:, pair * S + st * P:pair * S + (st + 1) * P],
                                    nn[w][:, 2 * (g % NG) + pair, :], start=(first and st == 0), stop=last,
                                    skip_group_check=True)
                ins.then_inc(p_out, 1)

            for g in range(2):
                for c in range(QT * g, QT * g + QT):
                    queries(c)
                if g == 0:
                    latent(0)
            scores(0)
            scores(1)
            for n in range(NHB):
                g, h = n // G, n % G
                turn_scores(n)
                if n >= 1:
                    context(n - 1)
                if n + 2 < NHB:
                    scores(n + 2)
                for c in tiles_at(n):
                    queries(c)
                if h == 1 and g + 1 < NGB:
                    latent(g + 1)
                if h == 2 and g >= 1:
                    turn_context(g - 1)
                if h == 3 and g >= 1:
                    project(g - 1)
            context(NHB - 1)
            turn_context(NGB - 1)
            project(NGB - 1)
            if STAGE < 4:
                return
            for s in range(NT // 2):
                pe.wait_ge(v_y3, 2 * s + 2)
                if s >= 2:
                    pe.wait_ge(a_yT3, s - 1)
                for it in range(TPB):
                    for kc in range(KC):
                        ins = TR(bank[s % 2][:, kc * S + it * P:kc * S + (it + 1) * P],
                                 y_sb[:, TPB * s + it, kc * P:(kc + 1) * P], identf[:, :])
                ins.then_inc(p_yT3, 1)
            pe.wait_ge(v_ct, NGB)
            for t in range(NT):
                pe.wait_ge(a_yT3, t // 2 + 1)
                for kc in range(KC):
                    ins = M(bank[2][:, t * NE:(t + 1) * NE], yt_f[:, kc, t * P:(t + 1) * P], gwt[:, kc, :],
                            start=(kc == 0), stop=(kc == KC - 1))
            ins.then_inc(p_lg, 1)
            pe.wait_ge(v_oh, 1)
            oh2 = ohs[:, :, :].rearrange("p a b -> p (a b)")
            M(bank[3][:, 0:NT * NE], trib[:, :], oh2, start=True, stop=False, skip_group_check=True)
            for j in range(1, NT):
                ins = M(bank[3][:, j * NE:NT * NE], onesb[:, :], oh2[:, 0:(NT - j) * NE], start=False,
                        stop=(j == NT - 1), skip_group_check=True)
            ins.then_inc(p_pos, 1)

            def turn_rows(e):
                pe.wait_ge(d_slot, 32 * (e + 1))
                if e == 0:
                    pe.wait_ge(a_el, 1)
                    pe.wait_ge(v_idx, 1)
                if e >= 1:
                    pe.wait_ge(a_bT, e)
                    pe.wait_ge(v_bT, e)
                for part in range(2):
                    o = bank[part][:, :].bitcast(F16)
                    for kc in range(KC):
                        for i in range(3):
                            w = min(P, CAP - P * i)
                            ins = TR(o[:, kc * CAP + i * P:kc * CAP + i * P + w],
                                     slots[0:w, i, part * D + kc * P:part * D + (kc + 1) * P], ident16[0:w, 0:w])
                    ins.then_inc(p_bT, 1)

            turn_rows(0)
            for e in range(NE):
                pe.wait_ge(a_bT, e + 1)
                pe.wait_ge(v_bT, e + 1)
                pe.wait_ge(v_we, 4 * (e + 1))
                for m in range(MH):
                    n = e * MH + m
                    if n >= 3:
                        pe.wait_ge(v_h, n - 2)
                    k = 0
                    for a, w in PASSES:
                        for kc in range(KC):
                            ins = M(bank[2 + n % 3][:, 0:CAP], we[0][w][:, e % 2, kc * EH + m * P:kc * EH + (m + 1) * P],
                                    bufT[:, a, kc * CAP:(kc + 1) * CAP], start=(k == 0), stop=(k == 5))
                            k += 1
                    ins.then_inc(p_h, 1)
                if e + 1 < NE:
                    turn_rows(e + 1)
                if e >= 1:
                    pe.wait_ge(v_oe, 3 * e)
                for m in range(MH):
                    pe.wait_ge(g_h, e * MH + m + 1)
                    for i in range(3):
                        r = min(P, CAP - P * i)
                        for k, (a, w) in enumerate(PASSES):
                            ins = M(bank[5 + i][0:r, 0:D], hs[a][:, m, i * P:i * P + r],
                                    we[1][w][:, e % 2, m * D:(m + 1) * D],
                                    start=(m == 0 and k == 0), stop=(m == MH - 1 and k == 2))
                        if m == MH - 1:
                            ins.then_inc(p_oe, 1)


def tables():
    def rot(length, dim):
        inv = (1.0 / np.float32(10000.0) ** (np.arange(0, dim, 2, dtype=np.float32) / np.float32(dim))).astype(np.float32)
        f = np.arange(length, dtype=np.float32)[:, None] * inv[None, :]
        return np.repeat(np.sin(f), 2, axis=-1), np.repeat(np.cos(f), 2, axis=-1)

    sin, cos = rot(S, DCQ)
    sign = np.where(np.arange(DCQ) < HALF, -1.0, 1.0).astype(np.float32)
    sin = sin * sign
    at = np.arange(G * HALF) % HALF
    both = [np.stack([t[:, at].T, t[:, at + HALF].T], axis=1) for t in (cos, sin)]
    cosq, sinq = [(b.reshape(QT, P, 2 * S).transpose(1, 0, 2) / np.float32(WS)).astype(np.float32) for b in both]
    ks, kc = rot(S, DC)
    ks = ks * np.where(np.arange(DC) < DC // 2, -1.0, 1.0).astype(np.float32)
    kcos, ksin = [t.reshape(TPB, P, DC).transpose(1, 0, 2).astype(np.float32) for t in (kc, ks)]
    eye = np.eye(P, dtype=np.float32)
    return {
        "cosq": cosq, "sinq": sinq, "kcos": kcos, "ksin": ksin, "identf": eye, "ident16": eye.astype(np.float16),
        "identb": eye.astype(mybir.dt.np(BF16)), "trib": np.triu(np.ones((P, P), np.float32), 1).astype(mybir.dt.np(BF16)),
        "spare": SLOTS + np.arange(P, dtype=np.float32).reshape(P, 1), "iota8": np.tile(np.arange(NE, dtype=np.float32), (P, 1)),
    }


def kernel(**inputs):
    import concourse.bacc as bacc
    from concourse.bass_utils import run_bass_kernel_spmd

    a = {k: np.asarray(v) for k, v in inputs.items()}
    zl = np.zeros((NG, 2, 4, 2, DC, P), np.float32)
    zr = np.zeros((NH // 2, 2, DC, 2, DC), np.float32)
    for g in range(NG):
        for half in range(2):
            for j in range(4):
                t, pair = (j + 1) // 2, j // 2
                for row in range(P):
                    h, i = divmod(t * P + row, HALF)
                    if h // 2 == pair:
                        zl[g, half, j, h % 2, :, row] = a["L1_xattn_W_qr"][G * g + h, half * HALF + i, :]
    for h in range(NH):
        zr[h // 2, h % 2, :, h % 2, :] = a["L1_xattn_W_kr"][h].T
    arrays = {
        "x": a["x"], "ctx": a["ctx_512"].reshape(T, DC), "ctxT": a["ctx_512"].reshape(T, DC).T,
        "g_xattn": a["g_xattn"], "g_ffn": a["g_ffn"],
        "W_kT": a["L0_xattn_W_k"].T, "b_k": a["L0_xattn_b_k"], "ln_gamma": a["L0_xattn_ln_gamma"],
        "ln_beta": a["L0_xattn_ln_beta"],
        "gate_wT": a["L0_ffn_gate_w"].T, "gate_b": a["L0_ffn_gate_b"], "val_wT": a["L0_ffn_val_w"].T,
        "val_b": a["L0_ffn_val_b"], "out_wT": a["L0_ffn_out_w"].T, "out_b": a["L0_ffn_out_b"],
        "Wq": a["L1_xattn_Wq"], "w_kc_q": a["L1_xattn_w_kc_q"], "w_kc_kv": a["L1_xattn_w_kc_kv"],
        "WoT": a["L1_xattn_Wo"].T, "ZL": zl.reshape(NG * 2 * 4, P, P), "ZR": zr.reshape(NH // 2, P, P),
        "gating_w": a["L1_ffn_gating_w"], "w1": a["L1_ffn_w1"], "w2": a["L1_ffn_w2"],
        "b1T": a["L1_ffn_b1"].reshape(NE * MH, P).T, "b2": a["L1_ffn_b2"],
        **tables(),
    }
    nc = bacc.Bacc("TRN2", target_bir_lowering=False, num_devices=1)
    feeds, aps = {}, {}
    for name, v in arrays.items():
        v = np.ascontiguousarray(v)
        feeds[f"in_{name}"] = v
        aps[name] = nc.dram_tensor(f"in_{name}", v.shape, mybir.dt.from_np(v.dtype), kind="ExternalInput").ap()
    out = nc.dram_tensor("out_x", (B, S, D), F32, kind="ExternalOutput").ap()
    program(nc, aps, out)
    r = run_bass_kernel_spmd(nc, [feeds], core_ids=[0])
    return r.results[0]["out_x"]
```

```python
from contextlib import ExitStack

import numpy as np
import concourse.bass as bass
from concourse import mybir

ALU = mybir.AluOpType
ACT = mybir.ActivationFunctionType
AX = mybir.AxisListType
F32 = mybir.dt.float32
F16 = mybir.dt.float16
BF16 = mybir.dt.bfloat16
U32 = mybir.dt.uint32

P = 128
B, S, D = 4, 256, 256
T = B * S
NT = T // P
TPB = S // P
KC = D // P
DC = 64
FH = 4 * D
NH, HK, DCQ = 16, 128, 192
HALF = DCQ // 2
G = 4
NG = NH // G
QT = G * HALF // P
NGB = B * NG
NHB = B * NH
NE, TOPK, EH = 8, 2, 1024
MH = EH // P
CAP = -(-T * TOPK * 5 // (NE * 4))
SLOTS = NE * CAP
WS = 64.0
MAGIC = 12582912.0
PASSES = ((0, 0), (0, 1), (1, 0))
def program(nc, A, out):
    ctx = ExitStack()
    with ctx:
        def sb(name, shape, dt=F32):
            return ctx.enter_context(nc.sbuf_tensor(name, shape, dt))

        def sem(name):
            return ctx.enter_context(nc.semaphore(name))

        def carve(arena, kb):
            at = [0]

            def take(shape, dt=F32):
                n = int(np.prod(shape)) * (4 if dt in (F32, U32) else 2) // 4
                a = arena[:, at[0]:at[0] + n]
                at[0] += n
                assert at[0] <= kb * 256, (at[0], kb)
                if dt != F32:
                    a = a.bitcast(dt)
                if len(shape) == 2:
                    a = a.rearrange("p (a b) -> p a b", a=shape[0])
                if len(shape) == 3:
                    a = a.rearrange("p (a b c) -> p a b c", a=shape[0], b=shape[1])
                return a
            return take

        bank = [ctx.enter_context(nc.psum_tensor(f"bank{i}", [P, 512], F32)) for i in range(8)]

        x_sb = sb("x_sb", [P, NT, D])
        y_sb = sb("y_sb", [P, NT, D])
        identf = sb("identf", [P, P])
        ident16 = sb("ident16", [P, P], F16)
        identb = sb("identb", [P, P], BF16)
        onesf = sb("onesf", [P, P])
        ctx_n = sb("ctx_n", [P, NT, DC])
        gx = sb("gx", [P, 2])
        gf = sb("gf", [P, 2])
        tgx = sb("tgx", [P, 2])
        tgf = sb("tgf", [P, 2])
        tgx1 = sb("tgx1", [P, 1])
        stats = sb("stats", [P, NT, 6])
        mv = sb("mv", [P, NT, 2])
        vareps = sb("vareps", [P, NT])
        mhalf = sb("mhalf", [P, NT])
        magic = sb("magic", [P, 1])
        rstd = sb("rstd", [P, NT])

        lp = carve(sb("lp", [P, 74 * 256]), 74)
        yt_f = lp([KC, T])
        yth = yt_f[:, 0, :].bitcast(F16).rearrange("p (a b) -> p a b", a=KC)
        ytl = yt_f[:, 1, :].bitcast(F16).rearrange("p (a b) -> p a b", a=KC)
        m1 = [lp([KC, 2, NH * HALF], F16) for _ in range(2)]
        zp = lp([NG * 2 * 4, P])
        nn = [lp([NH // 2, D], F16) for _ in range(2)]
        tabs = lp([2 * QT * 2 * S])
        cosq, sinq = [tabs[:, i * 2 * QT * S:(i + 1) * 2 * QT * S].rearrange("p (a b) -> p a b", a=QT) for i in range(2)]
        kvt = [lp([T], F16) for _ in range(2)]
        kvr = [lp([NT, DC], F16) for _ in range(2)]

        lw = sb("lw", [P, 34 * 256])
        se = sb("se", [P, 69 * 256])
        w0 = carve(lw, 34)
        outT = w0([T])
        kv0 = w0([NT, DC])
        kvT0 = w0([T])
        ctxT = w0([T])
        wkT = w0([DC])
        bkc = w0([1])
        bkb = w0([DC])
        gab = w0([D])
        beb = w0([D])
        z_sb = w0([NT, D])
        w0([30 * 256 - (2 * T + T + 512 + 64 + 1 + 64 + 2 * D + NT * D)])
        st_sb = w0([2, 512])
        stats2 = sb("stats2", [P, NT, 6])
        mv2 = sb("mv2", [P, NT, 2])
        ve2 = sb("ve2", [P, NT])
        rstd2 = sb("rstd2", [P, NT])
        nm0 = sb("nm0", [P, NT])
        sum0 = sb("sum0", [P, NT])
        r0 = sb("r0", [P, NT])
        w1 = carve(lw, 34)
        g_sb = w1([2, FH])
        v_sb = w1([2, FH])
        hq = w1([2, FH], BF16)
        hqT = w1([2, FH], BF16)
        q_sb = w1([NT, D], BF16)
        qT = w1([2, D], BF16)
        fo = w1([D])
        w2 = carve(lw, 34)
        raw = w2([2, 512])
        t1 = w2([2, 512])
        t2 = w2([2, 512])
        rope = w2([QT, 512])
        qz = [w2([2, 512], F16) for _ in range(2)]
        e_sb = w2([2, 512])
        at = [w2([2, 512], F16) for _ in range(2)]
        cxn = w2([512])
        ct = [w2([512], F16) for _ in range(2)]
        kvdup = raw.rearrange("p a b -> p (a b)").rearrange("p (t j d) -> p t j d", t=NT, j=2)
        nmax = sb("nmax", [P, 2, TPB])
        esum = sb("esum", [P, 2, TPB, G])
        rsum = sb("rsum", [P, 2, TPB, G])
        kcos = sb("kcos", [P, TPB, DC])
        ksin = sb("ksin", [P, TPB, DC])
        s1 = carve(se, 69)
        r1 = s1([28 * 256])
        r2 = s1([20 * 256])
        gb_b = s1([FH])
        vb_b = s1([FH])
        ob_b = s1([D])
        gtern = s1([KC, FH], BF16)
        vtern = s1([KC, FH], BF16)
        otern = s1([FH // P, D], BF16)
        wraw = [r1[:, 2048 * i:2048 * (i + 1)] for i in range(3)]
        wq = zp.rearrange("p a b -> p (a b)").rearrange("p (a b) -> p a b", a=NH)
        kcq = tabs.rearrange("p (a b) -> p a b", a=NH)
        zl = r1[:, 0:4096].rearrange("p (a b) -> p a b", a=NG * 2 * 4)
        zr = r1[:, 4096:5120].rearrange("p (a b) -> p a b", a=NH // 2)
        woT = r2[:, 0:4096].rearrange("p (a b) -> p a b", a=NH)
        kckv = r2[:, 4096:5120].rearrange("p (a b) -> p a b", a=NH)
        wabs = sb("wabs", [P, 3])
        gw = sb("gw", [P, 3])
        thr = sb("thr", [P, 3])
        nthr = sb("nthr", [P, 3])
        am = sb("am", [P, NT])
        qs = sb("qs", [P, NT])
        sgs = sb("sgs", [P, NT])
        svs = sb("svs", [P, NT])
        am2 = sb("am2", [P, NT])
        qs2 = sb("qs2", [P, NT])
        sos = sb("sos", [P, NT])
        s3 = carve(se, 69)
        eraw = s3([2, KC * EH])
        we = [[s3([2, KC * EH], F16) for _ in range(2)] for _ in range(2)]
        b2b = s3([NE, D])
        rows = s3([NT, 2 * D], F16)
        yt4 = s3([KC, S])
        got = eraw.rearrange("p a b -> p (a b)").rearrange("p (t k) -> p t k", t=NT)
        w3 = carve(lw, 34)
        slots = w3([3, 2 * D], F16)
        bufT = w3([2, KC * CAP], F16)
        hs = [w3([MH, CAP], F16) for _ in range(2)]
        hr = w3([2, CAP])
        oe = w3([6, D])
        b1s = sb("b1s", [P, NE * MH])
        b1w = sb("b1w", [P, NE * MH])
        gwt = sb("gwt", [P, KC, NE])
        trib = sb("trib", [P, P], BF16)
        onesb = sb("onesb", [P, P], BF16)
        iota8 = sb("iota8", [P, NE])
        spare = sb("spare", [P, 1])
        mx = sb("mx", [P, NT])
        el = sb("el", [P, NT, NE])
        es = sb("es", [P, NT])
        gates = sb("gates", [P, NT, NE])
        v8 = sb("v8", [P, NT, 8])
        i8 = sb("i8", [P, NT, 8], U32)
        idf = sb("idf", [P, NT, TOPK])
        oh = sb("oh", [P, NT, TOPK, NE])
        ohs = sb("ohs", [P, NT, NE], BF16)
        pr = sb("pr", [P, NT, TOPK, NE])
        pos = sb("pos", [P, NT, TOPK])
        val = sb("val", [P, NT, TOPK])
        base = sb("base", [P, NT, TOPK])
        sl = sb("sl", [P, NT, TOPK])
        sl2 = sb("sl2", [P, NT, TOPK])
        scat = sb("scat", [P, NT * TOPK], U32)
        gi = sb("gi", [P, NT, TOPK])
        gidx = sb("gidx", [P, NT * TOPK], U32)
        ws = sb("ws", [P, NT])
        wn = sb("wn", [P, NT, TOPK])
        zero = kvt[0][:, 0:2 * D]
        buf_d = nc.dram_tensor("dispatch", (SLOTS + P, 2 * D), F16).ap()
        oe_d = nc.dram_tensor("expert_rows", (SLOTS, D), F32).ap()

        x_v = A["x"].rearrange("b (h p) d -> p (b h) d", p=P)
        out_v = out.rearrange("b (h p) d -> p (b h) d", p=P)

        d_x, d_c, d_k, d_w, d_gb = sem("d_x"), sem("d_c"), sem("d_k"), sem("d_w"), sem("d_gb")
        d_n, d_m, d_z, d_t = sem("d_n"), sem("d_m"), sem("d_z"), sem("d_t")
        d_e, d_b, d_zero, d_scat, d_slot = sem("d_e"), sem("d_b"), sem("d_zero"), sem("d_scat"), sem("d_slot")
        d_oe, d_got, d_out = [sem(f"d_oe{i}") for i in range(6)], [sem(f"d_got{t}") for t in range(NT)], sem("d_out")
        c_dve, c_pool, c_act = sem("c_dve"), sem("c_pool"), sem("c_act")
        s_init = sem("s_init")
        s_stat, s_rstd, s_upd = sem("s_stat"), sem("s_rstd"), sem("s_upd")
        s_tanh = sem("s_tanh")
        p_kvT, a_kvT, p_kv, v_kv = sem("p_kvT"), sem("a_kvT"), sem("p_kv"), sem("v_kv")
        v_y0, p_yT0, a_yT0, p_oT, a_oT = sem("v_y0"), sem("p_yT0"), sem("a_yT0"), sem("p_oT"), sem("a_oT")
        p_sim, v_sst, g_srs, v_z, g_z, v_nm0, a_exp0 = (sem("p_sim"), sem("v_sst"), sem("g_srs"), sem("v_z"),
                                                       sem("g_z"), sem("v_nm0"), sem("a_exp0"))
        a_abs, p_abs, v_tern = sem("a_abs"), sem("p_abs"), sem("v_tern")
        v_q, p_qT, a_qT, p_gv, v_gv, a_silu = sem("v_q"), sem("p_qT"), sem("a_qT"), sem("p_gv"), sem("v_gv"), sem("a_silu")
        g_u, v_hq, p_hT, a_hT, p_fo, v_fo = sem("g_u"), sem("v_hq"), sem("p_hT"), sem("a_hT"), sem("p_fo"), sem("v_fo")
        v_qs2, a_rnd = sem("v_qs2"), sem("a_rnd")
        p_set, a_raws, a_set, g_set = sem("p_set"), sem("a_raws"), sem("a_set"), sem("g_set")
        v_y2, p_yT2, a_yT2, v_yT2 = sem("v_y2"), sem("p_yT2"), sem("a_yT2"), sem("v_yT2")
        v_kr, p_kr, a_kr, v_krl = sem("v_kr"), sem("p_kr"), sem("a_kr"), sem("v_krl")
        p_qb, a_raw, v_t1, g_t2, g_rope = sem("p_qb"), sem("a_raw"), sem("v_t1"), sem("g_t2"), sem("g_rope")
        p_qz, a_qz, v_qz = sem("p_qz"), sem("a_qz"), sem("v_qz")
        p_sc, v_max, a_exp, p_at, a_at, v_at, p_cx = (sem("p_sc"), sem("v_max"), sem("a_exp"), sem("p_at"),
                                                     sem("a_at"), sem("v_at"), sem("p_cx"))
        v_norm, p_ct, a_ct, v_ct, p_out = sem("v_norm"), sem("p_ct"), sem("a_ct"), sem("v_ct"), sem("p_out")
        v_y3, g_row, p_yT3, a_yT3, p_lg = sem("v_y3"), sem("g_row"), sem("p_yT3"), sem("a_yT3"), sem("p_lg")
        v_el, a_el, v_oh, p_pos, v_idx, v_gidx = sem("v_el"), sem("a_el"), sem("v_oh"), sem("p_pos"), sem("v_idx"), sem("v_gidx")
        a_we, v_we = sem("a_we"), sem("v_we")
        p_bT, a_bT, v_bT = sem("p_bT"), sem("a_bT"), sem("v_bT")
        p_h, a_h, v_h, g_h, p_oe, v_oe = sem("p_h"), sem("a_h"), sem("v_h"), sem("g_h"), sem("p_oe"), sem("v_oe")
        v_fin = sem("v_fin")

        UD = 5 * FH // 8
        NCONST = 16 * 13
        NSET = NH // 2 + NH + 8
        KB = NH // 2 + NH

        def unit(u):
            w = KC * DCQ if u < NH else D
            bk, st = bank[4 + u % 4][:, 0:w], st_sb[:, u % 2, 0:w]
            if u >= NH:
                return bk, st, [n[:, u - NH, :] for n in nn]
            bk, st = [x.rearrange("p (a b c) -> p a b c", a=KC, b=2) for x in (bk, st)]
            return bk, st, [m[:, :, :, u * HALF:(u + 1) * HALF] for m in m1]

        def tiles_at(n):
            g, h = n // G, n % G
            return [c for c in {2: [QT * (g + 2)], 3: [QT * (g + 2) + 1, QT * (g + 2) + 2]}.get(h, []) if c < QT * NGB]

        def routed(n, at):
            return [n // NH - 1] if n >= NH and n % NH == at else []

        def pair_of(b):
            return slice(TPB * b, TPB * b + TPB)

        block = ctx.enter_context(nc.Block())

        @block.sync
        def _(sp):
            for h in range(2):
                sp.dma_start(x_sb[:, 4 * h:4 * h + 4, :], x_v[:, 4 * h:4 * h + 4, :]).then_inc(d_x, 16)
            sp.dma_start(wraw[0].rearrange("p (a b) -> p a b", a=KC),
                         A["gate_wT"].rearrange("(a p) n -> p a n", p=P)).then_inc(d_w, 16)
            sp.wait_ge(d_w, 16)
            sp.dma_start(wraw[1].rearrange("p (a b) -> p a b", a=KC),
                         A["val_wT"].rearrange("(a p) n -> p a n", p=P)).then_inc(d_w, 16)
            sp.wait_ge(d_w, 32)
            sp.dma_start(wraw[2].rearrange("p (a b) -> p a b", a=FH // P),
                         A["out_wT"].rearrange("(a p) n -> p a n", p=P)).then_inc(d_w, 16)
            for dst, name in ((gb_b, "gate_b"), (vb_b, "val_b"), (ob_b, "out_b")):
                sp.dma_start(dst, A[name].partition_broadcast(P)).then_inc(d_gb, 16)
            sp.dma_start(wq, A["Wq"].rearrange("(h k) n -> k h n", k=P)).then_inc(d_m, 16)
            sp.dma_start(kcq, A["w_kc_q"].rearrange("h k n -> k h n")).then_inc(d_m, 16)
            sp.dma_start(woT, A["WoT"].rearrange("(h k) n -> k h n", k=P)).then_inc(d_n, 16)
            sp.dma_start(kckv, A["w_kc_kv"].rearrange("h k n -> k h n")).then_inc(d_n, 16)
            sp.wait_ge(v_tern, 3)
            sp.wait_ge(a_abs, 3)
            sp.dma_start(zl, A["ZL"].rearrange("a k n -> k a n")).then_inc(d_z, 16)
            sp.dma_start(zr, A["ZR"].rearrange("a k n -> k a n")).then_inc(d_z, 16)
            sp.wait_ge(s_init, 5)
            for i in range(SLOTS // P):
                sp.dma_start(buf_d[i * P:(i + 1) * P, :], zero).then_inc(d_zero, 16)
            sp.wait_ge(p_set, KB)
            sp.dma_start(cosq, A["cosq"]).then_inc(d_t, 16)
            sp.dma_start(sinq, A["sinq"]).then_inc(d_t, 16)
            sp.wait_ge(p_set, NSET)
            sp.wait_ge(v_fo, NT)
            sp.dma_start(b2b, A["b2"].partition_broadcast(P)).then_inc(d_b, 16)

            def weights(e):
                if e >= 1:
                    sp.wait_ge(v_we, 4 * e)
                sp.dma_start(eraw[:, 0, :].rearrange("p (a b) -> p a b", a=KC),
                             A["w1"][e].rearrange("(a p) n -> p a n", p=P)).then_inc(d_e, 16)
                sp.dma_start(eraw[:, 1, :].rearrange("p (a b) -> p a b", a=MH),
                             A["w2"][e].rearrange("(a p) n -> p a n", p=P)).then_inc(d_e, 16)

            def dispatched(e):
                if e == 0:
                    sp.wait_ge(d_scat, 16 * NT * TOPK)
                else:
                    sp.wait_ge(p_bT, 2 * e)
                sp.dma_start(slots[:, 0:2, :], buf_d[e * CAP:e * CAP + 2 * P, :].rearrange("(a p) c -> p a c", p=P))\
                    .then_inc(d_slot, 16)
                sp.dma_start(slots[0:CAP - 2 * P, 2, :], buf_d[e * CAP + 2 * P:(e + 1) * CAP, :]).then_inc(d_slot, 16)

            weights(0)
            weights(1)
            dispatched(0)
            for e in range(NE):
                if e + 1 < NE:
                    dispatched(e + 1)
                if e + 2 < NE:
                    weights(e + 2)
                for i in range(3):
                    k = 3 * e + i
                    w = min(P, CAP - P * i)
                    sp.wait_ge(v_oe, k + 1)
                    sp.dma_start(oe_d[e * CAP + P * i:e * CAP + P * i + w, :], oe[0:w, k % 6, :])\
                        .then_inc(d_oe[k % 6], 16)
            for t in range(NT):
                sp.wait_ge(v_fin, t + 1)
                sp.dma_start(out_v[:, t, :], x_sb[:, t, :]).then_inc(d_out, 16)
            sp.wait_ge(d_out, 16 * NT)

        @block.gpsimd
        def _(pool):
            chain = [0]

            def link(ins):
                chain[0] += 1
                ins.then_inc(c_pool, 1)
                pool.wait_ge(c_pool, chain[0])

            nc.gpsimd.memset(onesf[:, :], 1.0).then_inc(s_init, 1)
            nc.gpsimd.memset(onesb[:, :], 1.0).then_inc(s_init, 1)
            nc.gpsimd.memset(zero, 0.0).then_inc(s_init, 1)
            nc.gpsimd.memset(mhalf[:, :], -0.5).then_inc(s_init, 1)
            nc.gpsimd.memset(magic[:, :], MAGIC).then_inc(s_init, 1)
            pool.wait_ge(s_init, 5)
            def inv_std(a, b, stat, src, ve, dst, eps):
                link(nc.gpsimd.tensor_scalar(ve[:, a:b], src[:, a:b, 1], eps, None, ALU.add))
                nc.gpsimd.tensor_tensor(dst[:, a:b], ve[:, a:b], mhalf[:, a:b], ALU.pow).then_inc(stat, 1)

            pool.wait_ge(s_stat, 1)
            inv_std(0, NT, s_rstd, mv, vareps, rstd, 1e-5)
            for s in range(B + 1):
                if s < B:
                    pool.wait_ge(v_sst, s + 1)
                    inv_std(TPB * s, TPB * s + TPB, g_srs, mv2, ve2, rstd2, 1e-6)
                if s >= 1:
                    b = s - 1
                    pool.wait_ge(v_z, b + 1)
                    if b == 0:
                        pool.wait_ge(d_k, 96)
                    zz = z_sb[:, TPB * b:TPB * b + TPB, :]
                    link(nc.gpsimd.tensor_tensor(zz, zz, gab.unsqueeze(1).broadcast_to([P, TPB, D]), ALU.mult))
                    nc.gpsimd.tensor_tensor(zz, zz, beb.unsqueeze(1).broadcast_to([P, TPB, D]), ALU.add)\
                        .then_inc(g_z, 1)
            def set_low(u):
                pool.wait_ge(a_set, u + 1)
                _, src, dst = unit(u)
                nc.gpsimd.tensor_tensor(dst[1], src, dst[0], ALU.subtract).then_inc(g_set, 1)

            for u in range(KB // 2):
                set_low(u)
            pool.wait_ge(s_stat, 2)
            inv_std(0, NT, s_rstd, mv, vareps, rstd, 1e-5)
            for u in range(KB // 2, KB):
                set_low(u)

            def rows_std(b):
                pool.wait_ge(s_stat, 3 + b)
                inv_std(TPB * b, TPB * b + TPB, s_rstd, mv, vareps, rstd, 1e-5)

            for t in range(NT):
                pool.wait_ge(a_silu, t + 1)
                pool.wait_ge(v_gv, t + 1)
                nc.gpsimd.tensor_tensor(v_sb[:, t % 2, UD:FH], v_sb[:, t % 2, UD:FH], g_sb[:, t % 2, UD:FH], ALU.mult)\
                    .then_inc(g_u, 1)
                if t >= 2 and t % 2 == 0:
                    rows_std((t - 2) // 2)
            rows_std(B - 1)
            pool.wait_ge(d_t, 32)

            def rotate(c):
                pool.wait_ge(a_raw, c + 1)
                if c >= 2:
                    pool.wait_ge(g_rope, c - 1)
                r = raw[:, c % 2, :].rearrange("p (h s) -> p h s", h=2)
                sn = sinq[:, c % QT, :].rearrange("p (h s) -> p h s", h=2)
                o = t2[:, c % 2, :].rearrange("p (h s) -> p h s", h=2)
                nc.gpsimd.tensor_tensor(o[:, 0, :], r[:, 1, :], sn[:, 0, :], ALU.mult).then_inc(g_t2, 1)
                nc.gpsimd.tensor_tensor(o[:, 1, :], r[:, 0, :], sn[:, 1, :], ALU.mult).then_inc(g_t2, 1)
                pool.wait_ge(g_t2, 2 * c + 2)
                pool.wait_ge(v_t1, c + 1)
                if c >= QT:
                    pool.wait_ge(p_qz, c // QT)
                nc.gpsimd.tensor_tensor(rope[:, c % QT, :], t1[:, c % 2, :], t2[:, c % 2, :], ALU.add)\
                    .then_inc(g_rope, 1)

            def route_std(b):
                pool.wait_ge(s_stat, 3 + B + b)
                inv_std(TPB * b, TPB * b + TPB, s_rstd, mv, vareps, rstd, 1e-5)

            def route_rows(b):
                for t in (TPB * b, TPB * b + 1):
                    pool.wait_ge(v_y3, t + 1)
                    link(nc.gpsimd.tensor_copy(rows[:, t, 0:D], y_sb[:, t, :]))
                    nc.gpsimd.tensor_tensor(rows[:, t, D:2 * D], y_sb[:, t, :], rows[:, t, 0:D], ALU.subtract)\
                        .then_inc(g_row, 1)

            def route_out(b):
                pool.wait_ge(v_idx, b + 1)
                pool.wait_ge(g_row, TPB * (b + 1))
                for i in range(TPB * TOPK * b, TPB * TOPK * (b + 1)):
                    nc.gpsimd.indirect_dma_start(
                        out=buf_d[:, :], out_offset=bass.IndirectOffsetOnAxis(ap=scat[:, i:i + 1], axis=0),
                        in_=rows[:, i // TOPK, :], in_offset=None).then_inc(d_scat, 16)

            for c in range(2 * QT):
                rotate(c)
            for n in range(NHB):
                for c in tiles_at(n):
                    rotate(c)
                for b in routed(n, 3):
                    route_std(b)
                for b in routed(n, 4):
                    route_rows(b)
                for b in routed(n, 13):
                    route_out(b)
            route_std(B - 1)
            route_rows(B - 1)
            route_out(B - 1)
            for e in range(NE):
                for m in range(MH):
                    n = e * MH + m
                    pool.wait_ge(v_h, n + 1)
                    nc.gpsimd.tensor_tensor(hs[1][:, m, :], hr[:, n % 2, :], hs[0][:, m, :], ALU.subtract)\
                        .then_inc(g_h, 1)
            pool.wait_ge(v_we, 4 * NE)
            pool.wait_ge(a_we, 4 * NE)
            for r in range(6):
                pool.wait_ge(d_oe[r], 16 * NE // 2)
            pool.wait_ge(v_gidx, B)
            for i in range(NT * TOPK):
                nc.gpsimd.indirect_dma_start(
                    out=got[:, i // TOPK, (i % TOPK) * D:(i % TOPK + 1) * D], out_offset=None,
                    in_=oe_d[:, :], in_offset=bass.IndirectOffsetOnAxis(ap=gidx[:, i:i + 1], axis=0))\
                    .then_inc(d_got[i // TOPK], 16)

        @block.scalar
        def _(act):
            A_ = nc.scalar.activation
            act.dma_start(ctxT[0:DC, :], A["ctxT"]).then_inc(d_k, 16)
            act.dma_start(wkT[0:DC, :], A["W_kT"]).then_inc(d_k, 16)
            act.dma_start(bkc[0:DC, :], A["b_k"].rearrange("(p a) -> p a", a=1)).then_inc(d_k, 16)
            act.dma_start(gab, A["ln_gamma"].partition_broadcast(P)).then_inc(d_k, 16)
            act.dma_start(beb, A["ln_beta"].partition_broadcast(P)).then_inc(d_k, 16)
            act.dma_start(bkb, A["b_k"].partition_broadcast(P)).then_inc(d_k, 16)
            act.dma_start(identf[:, :], A["identf"]).then_inc(d_c, 16)
            act.dma_start(ident16[:, :], A["ident16"]).then_inc(d_c, 16)
            act.dma_start(identb[:, :], A["identb"]).then_inc(d_c, 16)
            act.dma_start(gx[:, :], A["g_xattn"].partition_broadcast(P)).then_inc(d_c, 16)
            act.dma_start(gf[:, :], A["g_ffn"].partition_broadcast(P)).then_inc(d_c, 16)
            act.dma_start(ctx_n[:, :, :], A["ctx"].rearrange("(t p) d -> p t d", p=P)).then_inc(d_c, 16)
            act.dma_start(kcos[:, :, :], A["kcos"]).then_inc(d_c, 16)
            act.dma_start(ksin[:, :, :], A["ksin"]).then_inc(d_c, 16)
            act.dma_start(b1s[:, :], A["b1T"]).then_inc(d_c, 16)
            act.dma_start(gwt[:, :, :], A["gating_w"].rearrange("(a p) n -> p a n", p=P)).then_inc(d_c, 16)
            act.dma_start(trib[:, :], A["trib"]).then_inc(d_c, 16)
            act.dma_start(iota8[:, :], A["iota8"]).then_inc(d_c, 16)
            act.dma_start(spare[:, :], A["spare"]).then_inc(d_c, 16)
            act.wait_ge(d_c, NCONST)
            act.wait_ge(s_init, 5)
            act.wait_ge(d_k, 16 * 6)
            A_(tgx[:, :], gx[:, :], ACT.Tanh).then_inc(s_tanh, 1)
            A_(tgf[:, :], gf[:, :], ACT.Tanh).then_inc(s_tanh, 1)
            for i in range(2):
                act.wait_ge(p_kvT, i + 1)
                A_(kvT0[0:DC, 512 * i:512 * i + 512], bank[i][0:DC, :], ACT.Identity, bias=bkc[0:DC, :])\
                    .then_inc(a_kvT, 1)
            for s in range(B + 3):
                if s < B:
                    act.wait_ge(p_yT0, s + 1)
                    A_(yt_f[:, :, s * S:(s + 1) * S], bank[4 + s % 2][:, :].rearrange("p (a b) -> p a b", a=KC),
                       ACT.Copy).then_inc(a_yT0, 1)
                if 1 <= s <= B:
                    b = s - 1
                    act.wait_ge(p_oT, b + 1)
                    A_(outT[0:DC, b * S:(b + 1) * S], bank[6 + b % 2][0:DC, 0:S], ACT.Copy, scale=1 / 16.0)\
                        .then_inc(a_oT, 1)
                if s in (1, 2, 3):
                    i = s - 1
                    act.wait_ge(d_w, 16 * (i + 1))
                    A_((gtern, vtern, otern)[i].rearrange("p a b -> p (a b)"), wraw[i], ACT.Abs, accum_out=wabs[:, i:i + 1]).then_inc(a_abs, 1)
                if s >= 3:
                    b = s - 3
                    act.wait_ge(v_nm0, b + 1)
                    for t in (TPB * b, TPB * b + 1):
                        A_(z_sb[:, t, :], z_sb[:, t, :], ACT.Exp, bias=nm0[:, t:t + 1], accum_out=sum0[:, t:t + 1])\
                            .then_inc(a_exp0, 1)
            for u in range(KB):
                act.wait_ge(p_set, u + 1)
                src, st, dst = unit(u)
                if u >= 2:
                    act.wait_ge(g_set, u - 1)
                A_(st, src, ACT.Copy, scale=WS).then_inc(a_raws, 1)
                A_(dst[0], src, ACT.Copy, scale=WS).then_inc(a_set, 1)

            def key_side(u):
                act.wait_ge(p_set, KB + u + 1)
                A_(zp[:, 4 * u:4 * u + 4, :], bank[7][:, :].rearrange("p (a b) -> p a b", a=4), ACT.Copy)\
                    .then_inc(a_set, 1)

            for s in range(NT + 2):
                for t in ([0, 1] if s == 0 else [s + 1] if s + 1 < NT else []):
                    act.wait_ge(p_qT, t + 1)
                    if t >= 2:
                        act.wait_ge(p_gv, t - 1)
                    A_(qT[:, t % 2, :], bank[0][:, 0:P].bitcast(BF16), ACT.Copy).then_inc(a_qT, 1)
                if s >= 2:
                    act.wait_ge(p_hT, s - 1)
                    A_(hqT[:, s % 2, :], bank[5][:, :].bitcast(BF16), ACT.Copy).then_inc(a_hT, 1)
                if s < NT:
                    act.wait_ge(v_gv, s + 1)
                    A_(g_sb[:, s % 2, :], g_sb[:, s % 2, :], ACT.Silu).then_inc(a_silu, 1)
                if s < NT:
                    key_side(s)
                if 1 <= s <= NT:
                    t = s - 1
                    act.wait_ge(v_qs2, t + 1)
                    A_(v_sb[:, t % 2, :], v_sb[:, t % 2, :], ACT.Identity, bias=magic[:, :], scale=qs2[:, t:t + 1])\
                        .then_inc(a_rnd, 1)
            act.wait_ge(d_zero, 16 * (SLOTS // P))
            for b in range(B):
                act.wait_ge(p_yT2, b + 1)
                A_(yth[:, :, b * S:(b + 1) * S], bank[b % 2][:, :].rearrange("p (a b) -> p a b", a=KC), ACT.Copy)\
                    .then_inc(a_yT2, 1)
            act.wait_ge(v_kr, 2)
            A_(kvr[0], kvdup[:, :, 0, :], ACT.Copy).then_inc(a_kr, 1)
            for i in range(2):
                act.wait_ge(p_kr, i + 1)
                A_(kvt[0][:, 512 * i:512 * i + 512], bank[2 + i][:, :], ACT.Copy).then_inc(a_kr, 1)

            def raw_copy(c):
                act.wait_ge(p_qb, c + 1)
                if c == 0:
                    act.wait_ge(v_krl, 1)
                if c >= 2:
                    act.wait_ge(g_t2, 2 * (c - 1))
                A_(raw[:, c % 2, :], bank[c % 2][:, :], ACT.Copy).then_inc(a_raw, 1)

            def qz_high(g):
                act.wait_ge(p_qz, g + 1)
                if g >= 2:
                    act.wait_ge(p_sc, G * (g - 1))
                A_(qz[0][:, g % 2, :], bank[2][:, :], ACT.Copy).then_inc(a_qz, 1)

            def exps(n):
                g, h = n // G, n % G
                act.wait_ge(v_max, n + 1)
                if n >= 2:
                    act.wait_ge(p_at, n - 1)
                if h == 0 and g >= 2:
                    act.wait_ge(v_norm, g - 1)
                for st in range(TPB):
                    A_(e_sb[:, n % 2, st * S:(st + 1) * S], bank[3 + n % 2][:, st * S:(st + 1) * S], ACT.Exp,
                       bias=nmax[:, n % 2, st:st + 1], accum_out=esum[:, g % 2, st, h:h + 1]).then_inc(a_exp, 1)

            def at_high(n):
                act.wait_ge(p_at, n + 1)
                if n >= 2:
                    act.wait_ge(p_cx, n - 1)
                A_(at[0][:, n % 2, :], bank[5][:, :], ACT.Copy).then_inc(a_at, 1)

            def ct_high(g):
                act.wait_ge(p_ct, g + 1)
                if g >= 1:
                    act.wait_ge(p_out, g)
                A_(ct[0], bank[2][:, :], ACT.Copy).then_inc(a_ct, 1)

            def split_high(k):
                e, q = k // 4, k % 4
                act.wait_ge(d_e, 32 * (e + 1))
                if e >= 2:
                    act.wait_ge(p_oe, 3 * (e - 1))
                A_(we[q // 2][0][:, e % 2, (q % 2) * EH:(q % 2 + 1) * EH],
                   eraw[:, q // 2, (q % 2) * EH:(q % 2 + 1) * EH], ACT.Copy, scale=WS).then_inc(a_we, 1)

            def route_turned(b):
                act.wait_ge(p_yT3, b + 1)
                if b >= 1:
                    act.wait_ge(p_lg, b)
                A_(yt4, bank[0][:, :].rearrange("p (a b) -> p a b", a=KC), ACT.Copy).then_inc(a_yT3, 1)

            def route_exp(b):
                act.wait_ge(v_el, b + 1)
                A_(el[:, pair_of(b), :], el[:, pair_of(b), :], ACT.Exp).then_inc(a_el, 1)

            for g in range(2):
                for c in range(QT * g, QT * g + QT):
                    raw_copy(c)
                if g == 0:
                    qz_high(0)
            exps(0)
            for n in range(NHB):
                g, h = n // G, n % G
                at_high(n)
                if n + 1 < NHB:
                    exps(n + 1)
                for c in tiles_at(n):
                    raw_copy(c)
                if h == 1 and g + 1 < NGB:
                    qz_high(g + 1)
                if h == 2 and g >= 1:
                    ct_high(g - 1)
                if n in (24, 28, 32, 36):
                    split_high((n - 24) // 4)
                for b in routed(n, 5):
                    route_turned(b)
                for b in routed(n, 10):
                    route_exp(b)
            ct_high(NGB - 1)
            route_turned(B - 1)
            route_exp(B - 1)

            def rows_high(e):
                act.wait_ge(p_bT, 2 * e + 1)
                if e >= 1:
                    act.wait_ge(p_h, MH * e)
                A_(bufT[:, 0, :], bank[0][:, :].bitcast(F16)[:, 0:KC * CAP], ACT.Copy).then_inc(a_bT, 1)

            rows_high(0)
            for e in range(NE):
                for m in range(MH):
                    n = e * MH + m
                    act.wait_ge(p_h, n + 1)
                    if m == 0 and e >= 1:
                        act.wait_ge(p_oe, 3 * e)
                    A_(hs[0][:, m, :], bank[2 + n % 3][:, 0:CAP], ACT.Relu, bias=b1w[:, n:n + 1]).then_inc(a_h, 1)
                if e + 1 < NE:
                    rows_high(e + 1)
                    for q in range(4):
                        split_high(4 * (e + 1) + q)

        @block.vector
        def _(dve):
            V = nc.vector
            chain = [0]

            def link(ins):
                chain[0] += 1
                ins.then_inc(c_dve, 1)
                dve.wait_ge(c_dve, chain[0])

            def normed(t, sig):
                V.tensor_scalar(y_sb[:, t, :], x_sb[:, t, :], mv[:, t, 0:1], rstd[:, t:t + 1],
                                ALU.subtract, ALU.mult).then_inc(sig, 1)

            def all_stats(k):
                for t in range(NT):
                    ins = V.bn_stats(stats[:, t, :], x_sb[:, t, :])
                link(ins)
                for t in range(NT):
                    ins = V.bn_aggr(mv[:, t, :], stats[:, t, :])
                ins.then_inc(s_stat, 1)
                dve.wait_ge(s_rstd, k)

            dve.wait_ge(d_x, 32)
            all_stats(1)
            for t in range(NT):
                normed(t, v_y0)
            dve.wait_ge(p_kv, 1)
            dve.wait_ge(d_k, 96)
            V.tensor_tensor(kv0, bank[2][:, :].rearrange("p (a b) -> p a b", a=NT),
                            bkb.unsqueeze(1).broadcast_to([P, NT, DC]), ALU.add).then_inc(v_kv, 1)

            def ternary(i, dst):
                if i == 0:
                    dve.wait_ge(p_abs, 1)
                    link(V.tensor_scalar(gw[:, :], bank[3][:, 0:3], 1.0 / (FH * D), 1e-5, ALU.mult, ALU.max))
                    V.tensor_scalar(thr[:, :], gw[:, :], 0.5, None, ALU.mult)
                    link(V.tensor_scalar(nthr[:, :], gw[:, :], -0.5, None, ALU.mult))
                link(V.tensor_scalar(dst, wraw[i], nthr[:, i:i + 1], None, ALU.is_lt))
                V.scalar_tensor_tensor(dst, wraw[i], thr[:, i:i + 1], dst, ALU.is_gt, ALU.subtract)\
                    .then_inc(v_tern, 1)

            for s in range(B + 3):
                if s < B:
                    dve.wait_ge(p_sim, s + 1)
                    sm = bank[s % 2][:, :].rearrange("p (a b) -> p a b", a=TPB)
                    for i in range(TPB):
                        ins = V.bn_stats(stats2[:, TPB * s + i, :], sm[:, i, :])
                    link(ins)
                    for i in range(TPB):
                        ins = V.bn_aggr(mv2[:, TPB * s + i, :], stats2[:, TPB * s + i, :])
                    ins.then_inc(v_sst, 1)
                    dve.wait_ge(g_srs, s + 1)
                    for i in range(TPB):
                        t = TPB * s + i
                        ins = V.tensor_scalar(z_sb[:, t, :], sm[:, i, :], mv2[:, t, 0:1], rstd2[:, t:t + 1],
                                              ALU.subtract, ALU.mult)
                    ins.then_inc(v_z, 1)
                if 1 <= s <= B:
                    b = s - 1
                    dve.wait_ge(g_z, b + 1)
                    V.tensor_reduce(nm0[:, TPB * b:TPB * b + TPB], z_sb[:, TPB * b:TPB * b + TPB, :], AX.X, ALU.max,
                                    negate=True).then_inc(v_nm0, 1)
                if s >= B:
                    ternary(s - B, (gtern, vtern, otern)[s - B].rearrange("p a b -> p (a b)"))
                if s >= 3:
                    b = s - 3
                    dve.wait_ge(a_exp0, TPB * (b + 1))
                    if b == 0:
                        dve.wait_ge(s_tanh, 2)
                    ts = slice(TPB * b, TPB * b + TPB)
                    link(V.reciprocal(r0[:, ts], sum0[:, ts]))
                    link(V.tensor_scalar(r0[:, ts], r0[:, ts], tgx[:, 0:1], None, ALU.mult))
                    for t in (TPB * b, TPB * b + 1):
                        V.scalar_tensor_tensor(x_sb[:, t, :], z_sb[:, t, :], r0[:, t:t + 1], x_sb[:, t, :],
                                               ALU.mult, ALU.add).then_inc(s_upd, 1)
            dve.wait_ge(s_upd, NT)
            all_stats(2)
            for t in range(NT):
                ins = V.tensor_scalar(y_sb[:, t, :], x_sb[:, t, :], mv[:, t, 0:1], rstd[:, t:t + 1],
                                      ALU.subtract, ALU.mult)
            link(ins)
            link(V.tensor_reduce(am[:, :], y_sb[:, :, :], AX.X, ALU.max, apply_absolute_value=True))
            link(V.tensor_scalar(am[:, :], am[:, :], 1e-5, None, ALU.max))
            link(V.reciprocal(qs[:, :], am[:, :]))
            link(V.tensor_scalar(qs[:, :], qs[:, :], 127.0, None, ALU.mult))
            V.tensor_scalar(sgs[:, :], am[:, :], gw[:, 0:1], 1 / 127.0, ALU.mult, ALU.mult)
            V.tensor_scalar(svs[:, :], am[:, :], gw[:, 1:2], 1 / 127.0, ALU.mult, ALU.mult)
            for t in range(NT):
                ins = V.tensor_scalar(y_sb[:, t, :], y_sb[:, t, :], qs[:, t:t + 1], MAGIC, ALU.mult, ALU.add)
            link(ins)
            for t in range(NT):
                V.tensor_scalar(q_sb[:, t, :], y_sb[:, t, :], MAGIC, 127.0, ALU.subtract, ALU.min).then_inc(v_q, 1)
            dve.wait_ge(d_gb, 48)

            def rotate_context():
                xr = ctx_n[:, :, :].rearrange("p (b i) d -> p b i d", b=B)
                yb = y_sb[:, 0:2, :].rearrange("p a b -> p (a b)")
                ya = yb.rearrange("p (b i d) -> p b i d", b=B, i=TPB)
                for b in range(B):
                    V.tensor_tensor(ya[:, b, :, 0:DC // 2], xr[:, b, :, DC // 2:DC], ksin[:, :, 0:DC // 2], ALU.mult)
                    ins = V.tensor_tensor(ya[:, b, :, DC // 2:DC], xr[:, b, :, 0:DC // 2], ksin[:, :, DC // 2:DC],
                                          ALU.mult)
                link(ins)
                for b in range(B):
                    ins = V.tensor_tensor(xr[:, b], xr[:, b], kcos[:, :, :], ALU.mult)
                link(ins)
                link(V.tensor_tensor(ctx_n[:, :, :], ctx_n[:, :, :], yb.rearrange("p (t d) -> p t d", t=NT), ALU.add))

            def stats_of(b):
                for t in (TPB * b, TPB * b + 1):
                    ins = V.bn_stats(stats[:, t, :], x_sb[:, t, :])
                link(ins)
                for t in (TPB * b, TPB * b + 1):
                    ins = V.bn_aggr(mv[:, t, :], stats[:, t, :])
                ins.then_inc(s_stat, 1)

            def norm_rows(b):
                dve.wait_ge(s_rstd, 3 + b)
                for t in (TPB * b, TPB * b + 1):
                    normed(t, v_y2)

            for s in range(NT + 2):
                if s < NT:
                    dve.wait_ge(p_gv, s + 1)
                    if s >= 2:
                        dve.wait_ge(v_hq, s - 1)
                    for i in range(2):
                        V.scalar_tensor_tensor(v_sb[:, s % 2, 512 * i:512 * i + 512], bank[3 + i][:, :], svs[:, s:s + 1],
                                               vb_b[:, 512 * i:512 * i + 512], ALU.mult, ALU.add)
                    for i in range(2):
                        ins = V.scalar_tensor_tensor(g_sb[:, s % 2, 512 * i:512 * i + 512], bank[1 + i][:, :],
                                                     sgs[:, s:s + 1], gb_b[:, 512 * i:512 * i + 512],
                                                     ALU.mult, ALU.add)
                    ins.then_inc(v_gv, 1)
                if 1 <= s <= NT:
                    t, r = s - 1, (s - 1) % 2
                    dve.wait_ge(a_silu, t + 1)
                    dve.wait_ge(v_gv, t + 1)
                    link(V.tensor_tensor(v_sb[:, r, 0:UD], v_sb[:, r, 0:UD], g_sb[:, r, 0:UD], ALU.mult))
                    dve.wait_ge(g_u, t + 1)
                    link(V.tensor_reduce(am2[:, t:t + 1], v_sb[:, r, :], AX.X, ALU.max, apply_absolute_value=True))
                    link(V.tensor_scalar(am2[:, t:t + 1], am2[:, t:t + 1], 1e-5, None, ALU.max))
                    link(V.reciprocal(qs2[:, t:t + 1], am2[:, t:t + 1]))
                    V.tensor_scalar(qs2[:, t:t + 1], qs2[:, t:t + 1], 127.0, None, ALU.mult).then_inc(v_qs2, 1)
                    V.tensor_scalar(sos[:, t:t + 1], am2[:, t:t + 1], gw[:, 2:3], 1 / 127.0, ALU.mult, ALU.mult)
                if s >= 2:
                    t = s - 2
                    dve.wait_ge(p_fo, t + 1)
                    dve.wait_ge(s_upd, NT + t)
                    V.scalar_tensor_tensor(fo, bank[6][:, 0:D], sos[:, t:t + 1], ob_b, ALU.mult, ALU.add)\
                        .then_inc(v_fo, 1)
                    dve.wait_ge(v_fo, t + 1)
                    V.scalar_tensor_tensor(x_sb[:, t, :], fo, tgf[:, 0:1], x_sb[:, t, :], ALU.mult, ALU.add)\
                        .then_inc(s_upd, 1)
                if 1 <= s <= NT:
                    t, r = s - 1, (s - 1) % 2
                    dve.wait_ge(a_rnd, t + 1)
                    if t >= 2:
                        dve.wait_ge(p_hT, t - 1)
                    V.tensor_scalar(hq[:, r, :], v_sb[:, r, :], MAGIC, 127.0, ALU.subtract, ALU.min).then_inc(v_hq, 1)
                if s == 2:
                    rotate_context()
                if s >= 3 and s % 2 == 1:
                    dve.wait_ge(s_upd, NT + s - 1)
                    stats_of((s - 3) // 2)
                if s >= 4 and s % 2 == 0:
                    norm_rows((s - 4) // 2)
            kt = kvdup
            dve.wait_ge(a_hT, NT)
            dve.wait_ge(p_fo, NT)
            for j in range(2):
                V.tensor_copy(kt[:, :, j, :], ctx_n[:, :, :]).then_inc(v_kr, 1)
            norm_rows(B - 1)
            for b in range(B):
                dve.wait_ge(a_yT2, b + 1)
                V.tensor_tensor(ytl[:, :, b * S:(b + 1) * S], bank[b % 2][:, :].rearrange("p (a b) -> p a b", a=KC),
                                yth[:, :, b * S:(b + 1) * S], ALU.subtract).then_inc(v_yT2, 1)
            dve.wait_ge(a_kr, 1)
            V.tensor_tensor(kvr[1], kt[:, :, 0, :], kvr[0], ALU.subtract).then_inc(v_krl, 1)
            for i in range(2):
                dve.wait_ge(a_kr, i + 2)
                V.tensor_tensor(kvt[1][:, 512 * i:512 * i + 512], bank[2 + i][:, :],
                                kvt[0][:, 512 * i:512 * i + 512], ALU.subtract).then_inc(v_krl, 1)
            V.tensor_scalar(tgx1[:, :], tgx[:, 1:2], 1.0 / WS, None, ALU.mult)
            dve.wait_ge(d_t, 32)

            def turn(c):
                dve.wait_ge(a_raw, c + 1)
                if c >= 2:
                    dve.wait_ge(g_rope, c - 1)
                V.tensor_tensor(t1[:, c % 2, :], bank[c % 2][:, :], cosq[:, c % QT, :], ALU.mult).then_inc(v_t1, 1)

            def qz_low(g):
                dve.wait_ge(a_qz, g + 1)
                V.tensor_tensor(qz[1][:, g % 2, :], bank[2][:, :], qz[0][:, g % 2, :], ALU.subtract).then_inc(v_qz, 1)

            def maxima(n):
                dve.wait_ge(p_sc, n + 1)
                if n >= 2:
                    dve.wait_ge(a_exp, TPB * (n - 1))
                V.tensor_reduce(nmax[:, n % 2, :], bank[3 + n % 2][:, :].rearrange("p (a b) -> p a b", a=TPB),
                                AX.X, ALU.max, negate=True).then_inc(v_max, 1)

            def at_low(n):
                dve.wait_ge(a_at, n + 1)
                V.tensor_tensor(at[1][:, n % 2, :], bank[5][:, :], at[0][:, n % 2, :], ALU.subtract).then_inc(v_at, 1)

            def norm(g):
                dve.wait_ge(a_exp, TPB * G * (g + 1))
                rs = rsum[:, g % 2].rearrange("p a b -> p (a b)")
                link(V.reciprocal(rs, esum[:, g % 2].rearrange("p a b -> p (a b)")))
                dve.wait_ge(p_cx, G * (g + 1))
                if g >= 1:
                    dve.wait_ge(p_ct, g)
                V.tensor_tensor(cxn.rearrange("p (a b) -> p a b", b=DC),
                                bank[6][:, :].rearrange("p (a b) -> p a b", b=DC),
                                rs.unsqueeze(2).broadcast_to([P, TPB * G, DC]), ALU.mult).then_inc(v_norm, 1)

            def ct_low(g):
                dve.wait_ge(a_ct, g + 1)
                V.tensor_tensor(ct[1], bank[2][:, :], ct[0], ALU.subtract).then_inc(v_ct, 1)

            def update(b):
                dve.wait_ge(p_out, NG * (b + 1))
                ts = slice(TPB * b, TPB * b + TPB)
                V.scalar_tensor_tensor(x_sb[:, ts, :], bank[7][:, :].rearrange("p (a b) -> p a b", a=TPB), tgx1[:, 0:1],
                                       x_sb[:, ts, :], ALU.mult, ALU.add).then_inc(s_upd, 1)

            def split_low(k):
                e, q = k // 4, k % 4
                part = slice((q % 2) * EH, (q % 2 + 1) * EH)
                dve.wait_ge(a_we, k + 1)
                V.scalar_tensor_tensor(we[q // 2][1][:, e % 2, part], eraw[:, q // 2, part], WS,
                                       we[q // 2][0][:, e % 2, part], ALU.mult, ALU.subtract).then_inc(v_we, 1)

            def route_stats(b):
                dve.wait_ge(s_upd, 2 * NT + b + 1)
                stats_of(b)

            def route_norm(b):
                dve.wait_ge(s_rstd, 3 + B + b)
                for t in (TPB * b, TPB * b + 1):
                    normed(t, v_y3)

            def route_logits(b):
                ts = pair_of(b)
                dve.wait_ge(p_lg, b + 1)
                lg = bank[0][:, 0:TPB * NE].rearrange("p (a b) -> p a b", a=TPB)
                link(V.tensor_reduce(mx[:, ts], lg, AX.X, ALU.max))
                V.tensor_tensor(el[:, ts, :], lg, mx[:, ts].unsqueeze(2).broadcast_to([P, TPB, NE]), ALU.subtract)\
                    .then_inc(v_el, 1)

            def route_pick(b):
                ts = pair_of(b)
                dve.wait_ge(a_el, b + 1)
                link(V.tensor_reduce(es[:, ts], el[:, ts, :], AX.X, ALU.add))
                link(V.reciprocal(es[:, ts], es[:, ts]))
                link(V.tensor_tensor(gates[:, ts, :], el[:, ts, :], es[:, ts].unsqueeze(2).broadcast_to([P, TPB, NE]),
                                     ALU.mult))
                for t in (TPB * b, TPB * b + 1):
                    ins = V.max(v8[:, t, :], gates[:, t, :])
                link(ins)
                for t in (TPB * b, TPB * b + 1):
                    ins = V.max_index(i8[:, t, :], v8[:, t, :], gates[:, t, :])
                link(ins)
                link(V.tensor_copy(idf[:, ts, :], i8[:, ts, 0:TOPK]))
                for k in range(TOPK):
                    ins = V.tensor_tensor(oh[:, ts, k, :], iota8[:, :].unsqueeze(1).broadcast_to([P, TPB, NE]),
                                          idf[:, ts, k].unsqueeze(2).broadcast_to([P, TPB, NE]), ALU.is_equal)
                link(ins)
                V.tensor_tensor(ohs[:, ts, :], oh[:, ts, 0, :], oh[:, ts, 1, :], ALU.add).then_inc(v_oh, 1)

            def route_place(b):
                ts = pair_of(b)
                js = slice(TPB * TOPK * b, TPB * TOPK * (b + 1))
                dve.wait_ge(p_pos, b + 1)
                cnt = bank[0][:, 0:TPB * NE].rearrange("p (a b) -> p a b", a=TPB)
                for k in range(TOPK):
                    ins = V.tensor_tensor(pr[:, ts, k, :], cnt, oh[:, ts, k, :], ALU.mult)
                link(ins)
                link(V.tensor_reduce(pos[:, ts, :], pr[:, ts, :, :], AX.X, ALU.add))
                V.tensor_scalar(val[:, ts, :], pos[:, ts, :], float(CAP), None, ALU.is_lt)
                link(V.tensor_scalar(base[:, ts, :], idf[:, ts, :], float(CAP), None, ALU.mult))
                link(V.tensor_tensor(sl[:, ts, :], pos[:, ts, :], base[:, ts, :], ALU.add))
                link(V.scalar_tensor_tensor(sl2[:, ts, :], sl[:, ts, :], spare[:, 0:1], val[:, ts, :],
                                            ALU.subtract, ALU.mult))
                V.tensor_scalar(scat[:, js], sl2[:, ts, :].rearrange("p a b -> p (a b)"), spare[:, 0:1], None, ALU.add)\
                    .then_inc(v_idx, 1)
                link(V.scalar_tensor_tensor(gi[:, ts, :], pos[:, ts, :], float(CAP - 1), base[:, ts, :],
                                            ALU.min, ALU.add))
                V.tensor_copy(gidx[:, js], gi[:, ts, :].rearrange("p a b -> p (a b)")).then_inc(v_gidx, 1)
                link(V.tensor_tensor(ws[:, ts], v8[:, ts, 0], v8[:, ts, 1], ALU.add))
                link(V.tensor_scalar(ws[:, ts], ws[:, ts], 1e-8, None, ALU.add))
                link(V.reciprocal(ws[:, ts], ws[:, ts]))
                link(V.tensor_tensor(wn[:, ts, :], v8[:, ts, 0:TOPK], ws[:, ts].unsqueeze(2).broadcast_to([P, TPB, TOPK]),
                                     ALU.mult))
                link(V.tensor_tensor(wn[:, ts, :], wn[:, ts, :], val[:, ts, :], ALU.mult))
                link(V.tensor_scalar(wn[:, ts, :], wn[:, ts, :], tgf[:, 1:2], None, ALU.mult))

            for g in range(2):
                for c in range(QT * g, QT * g + QT):
                    turn(c)
                if g == 0:
                    qz_low(0)
            maxima(0)
            maxima(1)
            for n in range(NHB):
                g, h = n // G, n % G
                at_low(n)
                if h == 0 and g >= 1:
                    norm(g - 1)
                if n + 2 < NHB:
                    maxima(n + 2)
                for c in tiles_at(n):
                    turn(c)
                if h == 1 and g + 1 < NGB:
                    qz_low(g + 1)
                if h == 2 and g >= 1:
                    ct_low(g - 1)
                if h == 3 and g >= 1 and g % NG == 0:
                    update(g // NG - 1)
                if n in (24, 28, 32, 36):
                    split_low((n - 24) // 4)
                for b in routed(n, 3):
                    route_stats(b)
                for b in routed(n, 4):
                    route_norm(b)
                for b in routed(n, 9):
                    route_logits(b)
                for b in routed(n, 11):
                    route_pick(b)
                for b in routed(n, 13):
                    route_place(b)
            norm(NGB - 1)
            ct_low(NGB - 1)
            update(B - 1)
            V.tensor_scalar(b1w[:, :], b1s[:, :], WS, None, ALU.mult)
            route_stats(B - 1)
            route_norm(B - 1)
            route_logits(B - 1)
            route_pick(B - 1)
            route_place(B - 1)
            dve.wait_ge(d_b, 16)

            def rows_low(e):
                dve.wait_ge(p_bT, 2 * e + 2)
                if e >= 1:
                    dve.wait_ge(p_h, MH * e)
                V.tensor_copy(bufT[:, 1, :], bank[1][:, :].bitcast(F16)[:, 0:KC * CAP]).then_inc(v_bT, 1)

            rows_low(0)
            for e in range(NE):
                for m in range(MH):
                    n = e * MH + m
                    dve.wait_ge(a_h, n + 1)
                    if n >= 2:
                        dve.wait_ge(g_h, n - 1)
                    V.tensor_scalar(hr[:, n % 2, :], bank[2 + n % 3][:, 0:CAP], b1w[:, n:n + 1], 0.0, ALU.add, ALU.max)\
                        .then_inc(v_h, 1)
                if e + 1 < NE:
                    rows_low(e + 1)
                    for q in range(4):
                        split_low(4 * (e + 1) + q)
                for i in range(3):
                    k = 3 * e + i
                    w = min(P, CAP - P * i)
                    dve.wait_ge(p_oe, k + 1)
                    if k >= 6:
                        dve.wait_ge(d_oe[k % 6], 16 * (k // 6))
                    V.scalar_tensor_tensor(oe[0:w, k % 6, :], bank[5 + i][0:w, 0:D], 1.0 / (WS * WS), b2b[0:w, e, :],
                                           ALU.mult, ALU.add).then_inc(v_oe, 1)
            for t in range(NT):
                dve.wait_ge(d_got[t], 16 * TOPK)
                link(V.scalar_tensor_tensor(x_sb[:, t, :], got[:, t, 0:D], wn[:, t, 0:1], x_sb[:, t, :],
                                            ALU.mult, ALU.add))
                V.scalar_tensor_tensor(x_sb[:, t, :], got[:, t, D:2 * D], wn[:, t, 1:2], x_sb[:, t, :],
                                       ALU.mult, ALU.add).then_inc(v_fin, 1)

        @block.tensor
        def _(pe):
            M = nc.tensor.matmul
            TR = nc.tensor.transpose
            pe.wait_ge(d_k, 96)
            for i in range(2):
                M(bank[i][0:DC, :], wkT[0:DC, :], ctxT[0:DC, 512 * i:512 * i + 512], start=True, stop=True)\
                    .then_inc(p_kvT, 1)
            for t in range(NT):
                ins = M(bank[2][:, t * DC:(t + 1) * DC], ctxT[0:DC, t * P:(t + 1) * P], wkT[0:DC, :],
                        start=True, stop=True)
            ins.then_inc(p_kv, 1)
            pe.wait_ge(d_c, NCONST)
            for s in range(B + 1):
                if s < B:
                    pe.wait_ge(v_y0, TPB * (s + 1))
                    if s >= 2:
                        pe.wait_ge(a_yT0, s - 1)
                    for it in range(TPB):
                        for jc in range(KC):
                            ins = TR(bank[4 + s % 2][:, jc * S + it * P:jc * S + (it + 1) * P],
                                     y_sb[:, TPB * s + it, jc * P:(jc + 1) * P], identf[:, :])
                    ins.then_inc(p_yT0, 1)
                if s >= 1:
                    b = s - 1
                    pe.wait_ge(a_yT0, b + 1)
                    if b == 0:
                        pe.wait_ge(v_kv, 1)
                    if b >= 2:
                        pe.wait_ge(a_oT, b - 1)
                    for jc in range(KC):
                        ins = M(bank[6 + b % 2][0:DC, 0:S], kv0[:, TPB * b + jc, :], yt_f[:, jc, b * S:(b + 1) * S],
                                start=(jc == 0), stop=(jc == KC - 1))
                    ins.then_inc(p_oT, 1)
                    pe.wait_ge(a_oT, b + 1)
                    if b == 0:
                        pe.wait_ge(a_kvT, 2)
                    if b >= 2:
                        pe.wait_ge(v_z, b - 1)
                    for it in range(TPB):
                        t = TPB * b + it
                        ins = M(bank[b % 2][:, it * S:(it + 1) * S], outT[0:DC, t * P:(t + 1) * P],
                                kvT0[0:DC, b * S:(b + 1) * S], start=True, stop=True)
                    ins.then_inc(p_sim, 1)
            pe.wait_ge(s_init, 5)
            pe.wait_ge(a_abs, 3)
            M(bank[3][:, 0:3], onesf[:, :], wabs[:, :], start=True, stop=True).then_inc(p_abs, 1)

            pe.wait_ge(a_oT, B)
            for u in range(KB):
                if u >= 4:
                    pe.wait_ge(a_set, u - 3)
                bk = bank[4 + u % 4]
                if u < NH:
                    if u == 0:
                        pe.wait_ge(d_m, 32)
                    for kc in range(KC):
                        ins = M(bk[:, kc * DCQ:(kc + 1) * DCQ], wq[:, u, kc * P:(kc + 1) * P], kcq[:, u, :],
                                start=True, stop=True)
                else:
                    if u == NH:
                        pe.wait_ge(d_n, 32)
                    for i in range(2):
                        h = 2 * (u - NH) + i
                        ins = M(bk[i * DC:(i + 1) * DC, 0:D], kckv[:, h, :], woT[:, h, :], start=True, stop=True)
                ins.then_inc(p_set, 1)

            def key_side(u):
                if u == 0:
                    pe.wait_ge(d_z, 32)
                pe.wait_ge(a_set, KB + u)
                for j in range(4):
                    k = 4 * u + j
                    ins = M(bank[7][:, j * P:(j + 1) * P], zl[:, k, :], zr[:, 2 * (k // 8) + j // 2, :],
                            start=True, stop=True)
                ins.then_inc(p_set, 1)

            def turn_q(t):
                pe.wait_ge(v_q, t + 1)
                if t >= 1:
                    pe.wait_ge(a_qT, t)
                for kc in range(KC):
                    ins = TR(bank[0][:, 0:P].bitcast(BF16)[:, kc * P:(kc + 1) * P], q_sb[:, t, kc * P:(kc + 1) * P],
                             identb[:, :])
                ins.then_inc(p_qT, 1)

            for s in range(NT + 2):
                if s == 0:
                    pe.wait_ge(v_z, B)
                    pe.wait_ge(a_oT, B)
                    pe.wait_ge(a_set, KB)
                    turn_q(0)
                if s < NT:
                    pe.wait_ge(a_qT, s + 1)
                    if s == 0:
                        pe.wait_ge(v_tern, 3)
                    if s >= 1:
                        pe.wait_ge(v_gv, s)
                    for w, o in ((vtern, 3), (gtern, 1)):
                        for i in range(2):
                            for kc in range(KC):
                                ins = M(bank[o + i][:, :], qT[:, s % 2, kc * P:(kc + 1) * P],
                                        w[:, kc, 512 * i:512 * i + 512], start=(kc == 0), stop=(kc == KC - 1))
                    ins.then_inc(p_gv, 1)
                    if s + 1 < NT:
                        turn_q(s + 1)
                    key_side(s)
                if s >= 2:
                    t = s - 2
                    pe.wait_ge(v_hq, t + 1)
                    if t >= 1:
                        pe.wait_ge(a_hT, t)
                    for j in range(FH // P):
                        ins = TR(bank[5][:, :].bitcast(BF16)[:, j * P:(j + 1) * P], hq[:, t % 2, j * P:(j + 1) * P],
                                 identb[:, :])
                    ins.then_inc(p_hT, 1)
                    pe.wait_ge(a_hT, t + 1)
                    if t >= 1:
                        pe.wait_ge(v_fo, t)
                    for j in range(FH // P):
                        ins = M(bank[6][:, 0:D], hqT[:, t % 2, j * P:(j + 1) * P], otern[:, j, :],
                                start=(j == 0), stop=(j == FH // P - 1))
                    ins.then_inc(p_fo, 1)
            for b in range(B):
                pe.wait_ge(v_y2, TPB * (b + 1))
                if b == 0:
                    pe.wait_ge(v_gv, NT)
                if b >= 2:
                    pe.wait_ge(v_yT2, b - 1)
                for it in range(TPB):
                    for kc in range(KC):
                        ins = TR(bank[b % 2][:, kc * S + it * P:kc * S + (it + 1) * P],
                                 y_sb[:, TPB * b + it, kc * P:(kc + 1) * P], identf[:, :])
                ins.then_inc(p_yT2, 1)
            pe.wait_ge(v_kr, 2)
            for i in range(2):
                for j in range(4):
                    ins = TR(bank[2 + i][:, j * P:(j + 1) * P], kvdup[:, 4 * i + j].rearrange("p a b -> p (a b)"),
                             identf[:, :])
                ins.then_inc(p_kr, 1)

            def queries(c):
                g, t = c // QT, c % QT
                b, col = g // NG, (g % NG) * G * HALF + t * P
                if c == 0:
                    pe.wait_ge(v_yT2, B)
                    pe.wait_ge(g_set, KB)
                if c >= 2:
                    pe.wait_ge(v_t1, c - 1)
                for half in range(2):
                    n = 0
                    for a, w in PASSES:
                        for kc in range(KC):
                            ins = M(bank[c % 2][:, half * S:(half + 1) * S], m1[w][:, kc, half, col:col + P],
                                    (yth, ytl)[a][:, kc, b * S:(b + 1) * S], start=(n == 0), stop=(n == 5))
                            n += 1
                ins.then_inc(p_qb, 1)

            def latent(g):
                pe.wait_ge(g_rope, QT * (g + 1))
                if g == 0:
                    pe.wait_ge(a_set, NSET)
                    pe.wait_ge(v_krl, 3)
                if g >= 1:
                    pe.wait_ge(v_qz, g)
                if g >= 3:
                    pe.wait_ge(v_ct, g - 2)
                for pair in range(2):
                    n = 0
                    for half in range(2):
                        for j in (2 * pair, 2 * pair + 1):
                            t = (j + 1) // 2
                            ins = M(bank[2][:, pair * S:(pair + 1) * S], zp[:, ((g % NG) * 2 + half) * 4 + j, :],
                                    rope[:, t, half * S:(half + 1) * S], start=(n == 0), stop=(n == 3))
                            n += 1
                ins.then_inc(p_qz, 1)

            def scores(n):
                g, h = n // G, n % G
                b, po, pair = n // NH, (h % 2) * DC, h // 2
                if h == 0:
                    pe.wait_ge(v_qz, g + 1)
                if n >= 2:
                    pe.wait_ge(a_exp, TPB * (n - 1))
                for st in range(TPB):
                    col = pair * S + st * P
                    for i, (a, w) in enumerate(PASSES):
                        ins = M(bank[3 + n % 2][:, st * S:(st + 1) * S], qz[a][po:po + DC, g % 2, col:col + P],
                                kvt[w][po:po + DC, b * S:(b + 1) * S], start=(i == 0), stop=(i == 2))
                ins.then_inc(p_sc, 1)

            def turn_scores(n):
                pe.wait_ge(a_exp, TPB * (n + 1))
                if n >= 1:
                    pe.wait_ge(v_at, n)
                for st in range(TPB):
                    for lt in range(TPB):
                        ins = TR(bank[5][:, lt * S + st * P:lt * S + (st + 1) * P],
                                 e_sb[:, n % 2, st * S + lt * P:st * S + (lt + 1) * P], identf[:, :])
                ins.then_inc(p_at, 1)

            def context(n):
                g, h, b = n // G, n % G, n // NH
                pe.wait_ge(v_at, n + 1)
                if h == 0 and g >= 1:
                    pe.wait_ge(v_norm, g)
                for st in range(TPB):
                    k = 0
                    for lt in range(TPB):
                        for a, w in PASSES:
                            ins = M(bank[6][:, st * S + h * DC:st * S + (h + 1) * DC],
                                    at[a][:, n % 2, lt * S + st * P:lt * S + (st + 1) * P],
                                    kvr[w][:, TPB * b + lt, :], start=(k == 0), stop=(k == 5))
                            k += 1
                ins.then_inc(p_cx, 1)

            def turn_context(g):
                pe.wait_ge(v_norm, g + 1)
                pe.wait_ge(v_qz, min(g + 3, NGB))
                for st in range(TPB):
                    for pair in range(2):
                        ins = TR(bank[2][:, pair * S + st * P:pair * S + (st + 1) * P],
                                 cxn[:, st * S + pair * P:st * S + (pair + 1) * P], identf[:, :])
                ins.then_inc(p_ct, 1)

            def project(g):
                b = g // NG
                pe.wait_ge(v_ct, g + 1)
                if g % NG == 0 and b >= 1:
                    pe.wait_ge(s_upd, 2 * NT + b)
                for pair in range(2):
                    for a, w in PASSES:
                        for st in range(TPB):
                            first = g % NG == 0 and pair == 0 and (a, w) == (0, 0)
                            last = g % NG == NG - 1 and pair == 1 and (a, w) == PASSES[-1]
                            ins = M(bank[7][:, st * S:(st + 1) * S], ct[a][:, pair * S + st * P:pair * S + (st + 1) * P],
                                    nn[w][:, 2 * (g % NG) + pair, :], start=(first and st == 0), stop=last,
                                    skip_group_check=True)
                ins.then_inc(p_out, 1)

            def route_turn(b):
                pe.wait_ge(v_y3, TPB * (b + 1))
                pe.wait_ge(v_t1, min(QT * (NG * (b + 1) + 3), QT * NGB))
                for it in range(TPB):
                    for kc in range(KC):
                        ins = TR(bank[0][:, kc * S + it * P:kc * S + (it + 1) * P],
                                 y_sb[:, TPB * b + it, kc * P:(kc + 1) * P], identf[:, :])
                ins.then_inc(p_yT3, 1)

            def route_logits(b):
                pe.wait_ge(a_yT3, b + 1)
                pe.wait_ge(v_t1, min(QT * (NG * (b + 1) + 4), QT * NGB))
                for t in range(TPB):
                    for kc in range(KC):
                        ins = M(bank[0][:, t * NE:(t + 1) * NE], yt4[:, kc, t * P:(t + 1) * P], gwt[:, kc, :],
                                start=(kc == 0), stop=(kc == KC - 1))
                ins.then_inc(p_lg, 1)

            def route_count(b):
                pe.wait_ge(v_oh, b + 1)
                pe.wait_ge(v_t1, min(QT * (NG * (b + 1) + 5), QT * NGB))
                oh2 = ohs[:, :, :].rearrange("p a b -> p (a b)")
                t0 = TPB * b
                M(bank[0][:, 0:TPB * NE], trib[:, :], oh2[:, t0 * NE:(t0 + TPB) * NE], start=True, stop=False,
                  skip_group_check=True)
                for j in range(t0):
                    M(bank[0][:, 0:TPB * NE], onesb[:, :], oh2[:, j * NE:(j + TPB) * NE], start=False, stop=False,
                      skip_group_check=True)
                M(bank[0][:, NE:2 * NE], onesb[:, :], oh2[:, 0:NE], start=False, stop=True,
                  skip_group_check=True).then_inc(p_pos, 1)

            for g in range(2):
                for c in range(QT * g, QT * g + QT):
                    queries(c)
                if g == 0:
                    latent(0)
            scores(0)
            scores(1)
            for n in range(NHB):
                g, h = n // G, n % G
                turn_scores(n)
                if n >= 1:
                    context(n - 1)
                if n + 2 < NHB:
                    scores(n + 2)
                for b in routed(n, 6):
                    pe.wait_ge(a_yT3, b + 1)
                for b in routed(n, 10):
                    pe.wait_ge(v_el, b + 1)
                for b in routed(n, 14):
                    pe.wait_ge(v_idx, b + 1)
                for c in tiles_at(n):
                    queries(c)
                if h == 1 and g + 1 < NGB:
                    latent(g + 1)
                if h == 2 and g >= 1:
                    turn_context(g - 1)
                if h == 3 and g >= 1:
                    project(g - 1)
                for b in routed(n, 5):
                    route_turn(b)
                for b in routed(n, 8):
                    route_logits(b)
                for b in routed(n, 12):
                    route_count(b)
            context(NHB - 1)
            turn_context(NGB - 1)
            project(NGB - 1)
            route_turn(B - 1)
            route_logits(B - 1)
            route_count(B - 1)

            def turn_rows(e):
                pe.wait_ge(d_slot, 32 * (e + 1))
                if e == 0:
                    pe.wait_ge(v_idx, B)
                if e >= 1:
                    pe.wait_ge(a_bT, e)
                    pe.wait_ge(v_bT, e)
                for part in range(2):
                    o = bank[part][:, :].bitcast(F16)
                    for kc in range(KC):
                        for i in range(3):
                            w = min(P, CAP - P * i)
                            ins = TR(o[:, kc * CAP + i * P:kc * CAP + i * P + w],
                                     slots[0:w, i, part * D + kc * P:part * D + (kc + 1) * P], ident16[0:w, 0:w])
                    ins.then_inc(p_bT, 1)

            turn_rows(0)
            for e in range(NE):
                pe.wait_ge(a_bT, e + 1)
                pe.wait_ge(v_bT, e + 1)
                pe.wait_ge(v_we, 4 * (e + 1))
                for m in range(MH):
                    n = e * MH + m
                    if n >= 3:
                        pe.wait_ge(v_h, n - 2)
                    k = 0
                    for a, w in PASSES:
                        for kc in range(KC):
                            ins = M(bank[2 + n % 3][:, 0:CAP], we[0][w][:, e % 2, kc * EH + m * P:kc * EH + (m + 1) * P],
                                    bufT[:, a, kc * CAP:(kc + 1) * CAP], start=(k == 0), stop=(k == 5))
                            k += 1
                    ins.then_inc(p_h, 1)
                if e + 1 < NE:
                    turn_rows(e + 1)
                if e >= 1:
                    pe.wait_ge(v_oe, 3 * e)
                for m in range(MH):
                    pe.wait_ge(g_h, e * MH + m + 1)
                    for i in range(3):
                        r = min(P, CAP - P * i)
                        for k, (a, w) in enumerate(PASSES):
                            ins = M(bank[5 + i][0:r, 0:D], hs[a][:, m, i * P:i * P + r],
                                    we[1][w][:, e % 2, m * D:(m + 1) * D],
                                    start=(m == 0 and k == 0), stop=(m == MH - 1 and k == 2))
                        if m == MH - 1:
                            ins.then_inc(p_oe, 1)


def tables():
    def rot(length, dim):
        inv = (1.0 / np.float32(10000.0) ** (np.arange(0, dim, 2, dtype=np.float32) / np.float32(dim))).astype(np.float32)
        f = np.arange(length, dtype=np.float32)[:, None] * inv[None, :]
        return np.repeat(np.sin(f), 2, axis=-1), np.repeat(np.cos(f), 2, axis=-1)

    sin, cos = rot(S, DCQ)
    sign = np.where(np.arange(DCQ) < HALF, -1.0, 1.0).astype(np.float32)
    sin = sin * sign
    at = np.arange(G * HALF) % HALF
    both = [np.stack([t[:, at].T, t[:, at + HALF].T], axis=1) for t in (cos, sin)]
    cosq, sinq = [(b.reshape(QT, P, 2 * S).transpose(1, 0, 2) / np.float32(WS)).astype(np.float32) for b in both]
    ks, kc = rot(S, DC)
    ks = ks * np.where(np.arange(DC) < DC // 2, -1.0, 1.0).astype(np.float32)
    kcos, ksin = [t.reshape(TPB, P, DC).transpose(1, 0, 2).astype(np.float32) for t in (kc, ks)]
    eye = np.eye(P, dtype=np.float32)
    return {
        "cosq": cosq, "sinq": sinq, "kcos": kcos, "ksin": ksin, "identf": eye, "ident16": eye.astype(np.float16),
        "identb": eye.astype(mybir.dt.np(BF16)), "trib": np.triu(np.ones((P, P), np.float32), 1).astype(mybir.dt.np(BF16)),
        "spare": SLOTS + np.arange(P, dtype=np.float32).reshape(P, 1), "iota8": np.tile(np.arange(NE, dtype=np.float32), (P, 1)),
    }


def kernel(**inputs):
    import concourse.bacc as bacc
    from concourse.bass_utils import run_bass_kernel_spmd

    a = {k: np.asarray(v) for k, v in inputs.items()}
    zl = np.zeros((NG, 2, 4, 2, DC, P), np.float32)
    zr = np.zeros((NH // 2, 2, DC, 2, DC), np.float32)
    for g in range(NG):
        for half in range(2):
            for j in range(4):
                t, pair = (j + 1) // 2, j // 2
                for row in range(P):
                    h, i = divmod(t * P + row, HALF)
                    if h // 2 == pair:
                        zl[g, half, j, h % 2, :, row] = a["L1_xattn_W_qr"][G * g + h, half * HALF + i, :]
    for h in range(NH):
        zr[h // 2, h % 2, :, h % 2, :] = a["L1_xattn_W_kr"][h].T
    arrays = {
        "x": a["x"], "ctx": a["ctx_512"].reshape(T, DC), "ctxT": a["ctx_512"].reshape(T, DC).T,
        "g_xattn": a["g_xattn"], "g_ffn": a["g_ffn"],
        "W_kT": a["L0_xattn_W_k"].T, "b_k": a["L0_xattn_b_k"], "ln_gamma": a["L0_xattn_ln_gamma"],
        "ln_beta": a["L0_xattn_ln_beta"],
        "gate_wT": a["L0_ffn_gate_w"].T, "gate_b": a["L0_ffn_gate_b"], "val_wT": a["L0_ffn_val_w"].T,
        "val_b": a["L0_ffn_val_b"], "out_wT": a["L0_ffn_out_w"].T, "out_b": a["L0_ffn_out_b"],
        "Wq": a["L1_xattn_Wq"], "w_kc_q": a["L1_xattn_w_kc_q"], "w_kc_kv": a["L1_xattn_w_kc_kv"],
        "WoT": a["L1_xattn_Wo"].T, "ZL": zl.reshape(NG * 2 * 4, P, P), "ZR": zr.reshape(NH // 2, P, P),
        "gating_w": a["L1_ffn_gating_w"], "w1": a["L1_ffn_w1"], "w2": a["L1_ffn_w2"],
        "b1T": a["L1_ffn_b1"].reshape(NE * MH, P).T, "b2": a["L1_ffn_b2"],
        **tables(),
    }
    nc = bacc.Bacc("TRN2", target_bir_lowering=False, num_devices=1)
    feeds, aps = {}, {}
    for name, v in arrays.items():
        v = np.ascontiguousarray(v)
        feeds[f"in_{name}"] = v
        aps[name] = nc.dram_tensor(f"in_{name}", v.shape, mybir.dt.from_np(v.dtype), kind="ExternalInput").ap()
    out = nc.dram_tensor("out_x", (B, S, D), F32, kind="ExternalOutput").ap()
    program(nc, aps, out)
    r = run_bass_kernel_spmd(nc, [feeds], core_ids=[0])
    return r.results[0]["out_x"]
```
